# Optimizing a Trainium2 kernel written in Bass

```python
import numpy as np
import jax
import jax.numpy as jnp

def _softmax(x, axis=-1):
    return jax.nn.softmax(x, axis=axis)

def _gelu(x):
    return jax.nn.gelu(x, approximate=True)

def _silu(x):
    return jax.nn.silu(x)

def _sigmoid(x):
    return jax.nn.sigmoid(x)

def _layernorm(x, axis=-1, eps=1e-05):
    m = jnp.mean(x, axis=axis, keepdims=True)
    v = jnp.var(x, axis=axis, keepdims=True)
    return (x - m) / jnp.sqrt(v + eps)

def _scatter_add(tgt, idx, src, axis=0):
    return tgt.at[idx].add(src)

def _segment_sum(src, seg, n):
    return jax.ops.segment_sum(src, seg, n)
kernel_name = 'mk_adj_preln_d4_adj_r2_317c12'

def setup_inputs(seed: int=0):
    np.random.seed(seed)
    _w = jnp.asarray

    def _rec_inputs():
        import jax
        import jax.numpy as jnp
        _gk = jax.random.key(seed)
        x = -0.0005207 + 1.001 * jax.random.normal(jax.random.fold_in(_gk, 1), (8, 1024, 128), jnp.float32)
        _a = jax.random.bernoulli(jax.random.fold_in(_gk, 2), 0.015625, (8, 1024, 1024))
        _a = jnp.logical_or(_a, jnp.swapaxes(_a, -1, -2))
        _a = jnp.logical_or(_a, jnp.eye(1024, dtype=bool))
        adj = _a.astype(jnp.int32)
        return (x, adj)
    x, adj = _rec_inputs()

    def _L0_gnn_setup():
        import jax, jax.numpy as jnp
        import numpy as np
        B, N, F_IN, F_OUT = (1, 4096, 128, 128)
        ALPHA = 0.2
        NEG_INF = -9000000000000000.0
        key = jax.random.key(seed)
        ks = jax.random.split(key, 8)
        feat = jax.random.normal(ks[0], (B, N, F_IN), dtype=jnp.float32)
        adj = jax.random.randint(ks[1], (B, N, N), 0, 2, dtype=jnp.int32)
        s = 1.414 * (6.0 / (F_IN + F_OUT)) ** 0.5
        W = jax.random.uniform(ks[2], (F_IN, F_OUT), minval=-s, maxval=s, dtype=jnp.float32)
        a_1 = jax.random.normal(ks[3], (F_OUT, 1), dtype=jnp.float32) * 0.1
        a_2 = jax.random.normal(ks[4], (F_OUT, 1), dtype=jnp.float32) * 0.1
        a_12 = jax.random.normal(ks[5], (F_OUT, F_OUT), dtype=jnp.float32) * (1.0 / F_OUT ** 0.5)
        W_1 = jax.random.uniform(ks[6], (F_IN, F_OUT), minval=-s, maxval=s, dtype=jnp.float32)
        W_2 = jax.random.uniform(ks[7], (F_IN, F_OUT), minval=-s, maxval=s, dtype=jnp.float32)
        return {'feat': feat, 'adj': adj, 'W': W, 'a_1': a_1, 'a_2': a_2, 'a_12': a_12, 'W_1': W_1, 'W_2': W_2}
    _L0_gnn_all = _L0_gnn_setup()
    _L0_gnn_in = {k: v for k, v in _L0_gnn_all.items() if k in ('W', 'a_1', 'a_2', 'a_12', 'W_1', 'W_2')}
    del _L0_gnn_all

    def _L1_gnn_setup():
        import jax, jax.numpy as jnp
        import numpy as np
        OUT = 128
        NUM_LAYERS = 3

        def _gru_cell(inp, h, w_ih, w_hh, b_ih, b_hh):
            gi = inp @ w_ih.T + b_ih
            gh = h @ w_hh.T + b_hh
            i_r, i_z, i_n = jnp.split(gi, 3, axis=-1)
            h_r, h_z, h_n = jnp.split(gh, 3, axis=-1)
            r = jax.nn.sigmoid(i_r + h_r)
            z = jax.nn.sigmoid(i_z + h_z)
            n = jnp.tanh(i_n + r * h_n)
            return (1.0 - z) * n + z * h
        key = jax.random.key(seed)
        ks = jax.random.split(key, 8)
        B, N, D = (32, 256, 128)
        x = jax.random.normal(ks[0], (B, N, D), dtype=jnp.float32)
        adj = jax.random.randint(ks[1], (B, N, N), 0, 2, dtype=jnp.int32)
        s = 1.0 / np.sqrt(OUT)
        weight = jax.random.uniform(ks[2], (NUM_LAYERS, OUT, OUT), jnp.float32, -s, s)
        w_ih = jax.random.uniform(ks[3], (3 * OUT, OUT), jnp.float32, -s, s)
        w_hh = jax.random.uniform(ks[4], (3 * OUT, OUT), jnp.float32, -s, s)
        b_ih = jax.random.uniform(ks[5], (3 * OUT,), jnp.float32, -s, s)
        b_hh = jax.random.uniform(ks[6], (3 * OUT,), jnp.float32, -s, s)
        return {'x': x, 'adj': adj, 'weight': weight, 'w_ih': w_ih, 'w_hh': w_hh, 'b_ih': b_ih, 'b_hh': b_hh}
    _L1_gnn_all = _L1_gnn_setup()
    _L1_gnn_in = {k: v for k, v in _L1_gnn_all.items() if k in ('weight', 'w_ih', 'w_hh', 'b_ih', 'b_hh')}
    del _L1_gnn_all

    def _L2_gnn_setup():
        import jax, jax.numpy as jnp
        import numpy as np
        NEG_BIG = -9000000000000000.0
        key = jax.random.key(seed)
        k_h, k_adj, k_W, k_a = jax.random.split(key, 4)
        B, N, F_in, F_out = (8, 1024, 128, 128)
        h = jax.random.normal(k_h, (B, N, F_in), dtype=jnp.float32)
        adj = jax.random.randint(k_adj, (B, N, N), 0, 2, dtype=jnp.int32)
        gain = 1.414
        lim_W = gain * np.sqrt(6.0 / (F_in + F_out))
        W = jax.random.uniform(k_W, (F_in, F_out), dtype=jnp.float32, minval=-lim_W, maxval=lim_W)
        lim_a = gain * np.sqrt(6.0 / (2 * F_out + 1))
        a = jax.random.uniform(k_a, (2 * F_out, 1), dtype=jnp.float32, minval=-lim_a, maxval=lim_a)
        return {'h': h, 'adj': adj, 'W': W, 'a': a}
    _L2_gnn_all = _L2_gnn_setup()
    _L2_gnn_in = {k: v for k, v in _L2_gnn_all.items() if k in ('W', 'a')}
    del _L2_gnn_all

    def _L3_gnn_setup():
        import jax, jax.numpy as jnp
        import numpy as np
        B, N, IN_F, OUT_F = (8, 1024, 128, 128)
        ALPHA = 0.2
        NEG_INF = -1000000000.0
        key = jax.random.key(seed)
        ks = jax.random.split(key, 8)
        h = jax.random.normal(ks[0], (B, N, IN_F), dtype=jnp.float32)
        adj = jax.random.randint(ks[1], (B, N, N), 0, 2, dtype=jnp.int32)
        W_w = jax.random.normal(ks[2], (OUT_F, IN_F), dtype=jnp.float32) * (1.414 / np.sqrt(IN_F + OUT_F))
        W_b = jnp.zeros((OUT_F,), dtype=jnp.float32)
        ai_w = jax.random.normal(ks[3], (1, OUT_F), dtype=jnp.float32) * (1.414 / np.sqrt(OUT_F + 1))
        ai_b = jnp.zeros((1,), dtype=jnp.float32)
        aj_w = jax.random.normal(ks[4], (1, OUT_F), dtype=jnp.float32) * (1.414 / np.sqrt(OUT_F + 1))
        aj_b = jnp.zeros((1,), dtype=jnp.float32)
        return {'h': h, 'adj': adj, 'W_w': W_w, 'W_b': W_b, 'ai_w': ai_w, 'ai_b': ai_b, 'aj_w': aj_w, 'aj_b': aj_b}
    _L3_gnn_all = _L3_gnn_setup()
    _L3_gnn_in = {k: v for k, v in _L3_gnn_all.items() if k in ('W_w', 'W_b', 'ai_w', 'ai_b', 'aj_w', 'aj_b')}
    del _L3_gnn_all
    return {'x': x, 'adj': adj, 'L0_gnn_W': _L0_gnn_in['W'], 'L0_gnn_a_1': _L0_gnn_in['a_1'], 'L0_gnn_a_2': _L0_gnn_in['a_2'], 'L0_gnn_a_12': _L0_gnn_in['a_12'], 'L0_gnn_W_1': _L0_gnn_in['W_1'], 'L0_gnn_W_2': _L0_gnn_in['W_2'], 'L1_gnn_weight': _L1_gnn_in['weight'], 'L1_gnn_w_ih': _L1_gnn_in['w_ih'], 'L1_gnn_w_hh': _L1_gnn_in['w_hh'], 'L1_gnn_b_ih': _L1_gnn_in['b_ih'], 'L1_gnn_b_hh': _L1_gnn_in['b_hh'], 'L2_gnn_W': _L2_gnn_in['W'], 'L2_gnn_a': _L2_gnn_in['a'], 'L3_gnn_W_w': _L3_gnn_in['W_w'], 'L3_gnn_W_b': _L3_gnn_in['W_b'], 'L3_gnn_ai_w': _L3_gnn_in['ai_w'], 'L3_gnn_ai_b': _L3_gnn_in['ai_b'], 'L3_gnn_aj_w': _L3_gnn_in['aj_w'], 'L3_gnn_aj_b': _L3_gnn_in['aj_b']}

def reference(x, adj, L0_gnn_W, L0_gnn_a_1, L0_gnn_a_2, L0_gnn_a_12, L0_gnn_W_1, L0_gnn_W_2, L1_gnn_weight, L1_gnn_w_ih, L1_gnn_w_hh, L1_gnn_b_ih, L1_gnn_b_hh, L2_gnn_W, L2_gnn_a, L3_gnn_W_w, L3_gnn_W_b, L3_gnn_ai_w, L3_gnn_ai_b, L3_gnn_aj_w, L3_gnn_aj_b):
    import jax
    import jax.numpy as jnp

    def _L0_gnn_ref(feat, adj, W, a_1, a_2, a_12, W_1, W_2):
        import jax, jax.numpy as jnp
        import numpy as np
        B, N, F_IN, F_OUT = (1, 4096, 128, 128)
        ALPHA = 0.2
        NEG_INF = -9000000000000000.0
        h = jnp.matmul(feat, W)
        Ax = jnp.matmul(h, a_1)
        Ay = jnp.matmul(h, a_2)
        A_xy = jnp.matmul(jnp.matmul(h, a_12), jnp.swapaxes(h, 1, 2))
        logits = jnp.swapaxes(Ax, 1, 2) + Ay + A_xy
        e = jax.nn.leaky_relu(logits, negative_slope=ALPHA)
        e = jnp.where(adj > 0, e, NEG_INF)
        attention = jax.nn.softmax(e, axis=-1)
        h_prime = jnp.matmul(attention, feat)
        h_out = jnp.matmul(feat, W_1) + jnp.matmul(h_prime, W_2)
        return jax.nn.elu(h_out)

    def _L1_gnn_ref(x, adj, weight, w_ih, w_hh, b_ih, b_hh):
        import jax, jax.numpy as jnp
        import numpy as np
        OUT = 128
        NUM_LAYERS = 3

        def _gru_cell(inp, h, w_ih, w_hh, b_ih, b_hh):
            gi = inp @ w_ih.T + b_ih
            gh = h @ w_hh.T + b_hh
            i_r, i_z, i_n = jnp.split(gi, 3, axis=-1)
            h_r, h_z, h_n = jnp.split(gh, 3, axis=-1)
            r = jax.nn.sigmoid(i_r + h_r)
            z = jax.nn.sigmoid(i_z + h_z)
            n = jnp.tanh(i_n + r * h_n)
            return (1.0 - z) * n + z * h
        A = (adj != 0).astype(x.dtype)
        h = x
        L = weight.shape[0]
        for i in range(L):
            m = jnp.einsum('bnd,de->bne', h, weight[i])
            aggr = jnp.einsum('bst,bsd->btd', A, m)
            h = _gru_cell(aggr, h, w_ih, w_hh, b_ih, b_hh)
        return h

    def _L2_gnn_ref(h, adj, W, a):
        import jax, jax.numpy as jnp
        import numpy as np
        NEG_BIG = -9000000000000000.0
        F_out = W.shape[1]
        Wh = jnp.matmul(h, W)
        a1 = a[:F_out, 0]
        a2 = a[F_out:, 0]
        e = (Wh @ a1)[:, :, None] + (Wh @ a2)[:, None, :]
        masked = jnp.where(adj > 0, e, jnp.float32(NEG_BIG))
        attention = jax.nn.softmax(masked, axis=-1)
        h_prime = jnp.matmul(attention, Wh)
        return jax.nn.elu(h_prime)

    def _L3_gnn_ref(h, adj, W_w, W_b, ai_w, ai_b, aj_w, aj_b):
        import jax, jax.numpy as jnp
        import numpy as np
        B, N, IN_F, OUT_F = (8, 1024, 128, 128)
        ALPHA = 0.2
        NEG_INF = -1000000000.0
        Wh = jnp.einsum('bni,oi->bno', h, W_w) + W_b
        Wh1 = jnp.einsum('bnf,of->bno', Wh, ai_w) + ai_b
        Wh2 = jnp.einsum('bnf,of->bno', Wh, aj_w) + aj_b
        e = Wh1 + jnp.swapaxes(Wh2, 1, 2)
        e = jnp.where(e >= 0, e, ALPHA * e)
        attention = jnp.where(adj > 0, e, NEG_INF)
        attention = jax.nn.softmax(attention, axis=2)
        h_hat = jnp.einsum('bnm,bmf->bnf', attention, Wh)
        return jax.nn.elu(h_hat)
    h = jnp.maximum(_layernorm(x, axis=-1), 0.0)
    x = x + _L0_gnn_ref(h, adj, L0_gnn_W, L0_gnn_a_1, L0_gnn_a_2, L0_gnn_a_12, L0_gnn_W_1, L0_gnn_W_2)
    h = jnp.maximum(_layernorm(x, axis=-1), 0.0)
    x = x + _L1_gnn_ref(h, adj, L1_gnn_weight, L1_gnn_w_ih, L1_gnn_w_hh, L1_gnn_b_ih, L1_gnn_b_hh)
    h = jnp.maximum(_layernorm(x, axis=-1), 0.0)
    x = x + _L2_gnn_ref(h, adj, L2_gnn_W, L2_gnn_a)
    h = jnp.maximum(_layernorm(x, axis=-1), 0.0)
    x = x + _L3_gnn_ref(h, adj, L3_gnn_W_w, L3_gnn_W_b, L3_gnn_ai_w, L3_gnn_ai_b, L3_gnn_aj_w, L3_gnn_aj_b)
    return x

_drawn_inputs = setup_inputs


def setup_inputs(seed=0):
    import zlib

    import numpy as np

    out = dict(_drawn_inputs(seed))
    spreads = {'L3_gnn_W_b': (0.0, 0.1)}
    factors = {'L0_gnn_a_2': 21.517, 'L3_gnn_ai_w': 17.652}
    for name, (base, spread) in spreads.items():
        noise = np.random.default_rng([zlib.crc32(name.encode()), seed]).standard_normal(out[name].shape)
        drawn = base * np.exp(spread * noise) if base else spread * noise
        out[name] = jnp.asarray(drawn.astype(out[name].dtype))
    for name, factor in factors.items():
        out[name] = (out[name] * factor).astype(out[name].dtype)
    return out
```

```python
from contextlib import ExitStack

import numpy as np

import concourse.bass as bass
from concourse import mybir
from concourse.alu_op_type import AluOpType as ALU

ACT = mybir.ActivationFunctionType
F32 = mybir.dt.float32
F32R = mybir.dt.float32r
BF16 = mybir.dt.bfloat16
I32 = mybir.dt.int32

P = 128
HALF = 512
MASKED = -9.0e15
LOWEST = -3.0e38
EPS = 1e-5
ALPHA = 0.2
STEEP = (1.0 - ALPHA) / ALPHA


class Steps:

    def __init__(self, sem, counts):
        self.sem, self.counts, self.n = sem, counts, 0

    def done(self, *step):
        self.n += 1
        self.counts[step] = self.n
        return self.sem, 1

    def at(self, *step):
        return self.sem, self.counts.get(step, 1)

    def last(self):
        return self.sem, self.n


def build(nc, counts, x, adj, p0, p1, p2, p3, out):
    GRAPHS, N, D = x.shape
    T = N // P
    H = N // HALF
    TH = T // H
    PAIRS = GRAPHS // 2
    GRU_LAYERS = p1["weight"].shape[0]
    VW = D + 1
    CHUNK = 2
    CHUNKS = T // CHUNK
    SLOTS = range(2)
    assert D == P and GRAPHS % 2 == 0

    with ExitStack() as ctx:
        def sb(name, shape, dt=F32):
            return ctx.enter_context(nc.sbuf_tensor(name, shape, dt))

        def sem(name):
            return ctx.enter_context(nc.semaphore(name))

        def steps(name):
            return Steps(sem(name), counts.setdefault(name, {}))

        edge_bytes = T * N * 4
        base = (nc.sbuf_base + 31) // 32 * 32
        slab = sb("edge_slab", [P, 2 * edge_bytes // 4 + 8], I32)
        adj_in = [nc.alloc_sbuf_tensor_at(f"adj_in{k}", [P, T, N], I32, offset=base + k * edge_bytes) for k in SLOTS]
        edges = [nc.alloc_sbuf_tensor_at(f"edges{k}", [P, T, N], F32R, offset=base + k * edge_bytes) for k in SLOTS]

        mask = [sb(f"mask{k}", [P, T, N], BF16) for k in SLOTS]
        xs = [sb(f"xs{k}", [P, T, D]) for k in SLOTS]
        hT = [sb(f"hT{k}", [P, N]) for k in SLOTS]
        hT_hi = [sb(f"hT_hi{k}", [P, N], F32R) for k in SLOTS]
        hT_lo = [sb(f"hT_lo{k}", [P, N], F32R) for k in SLOTS]
        part_hi = [sb(f"part_hi{k}", [P, N], F32R) for k in SLOTS]
        part_lo = [sb(f"part_lo{k}", [P, N], F32R) for k in SLOTS]
        vals = [sb(f"vals{k}", [P, T * VW]) for k in SLOTS]
        extra = [sb(f"extra{k}", [P, N]) for k in SLOTS]
        rows_j = [sb(f"rows_j{k}", [P, N], F32R) for k in SLOTS]
        rows_i = [sb(f"rows_i{k}", [P, N], F32R) for k in SLOTS]
        rows_c = [sb(f"rows_c{k}", [64, N], F32R) for k in SLOTS]
        h_nat = sb("h_nat", [P, T, D])
        RING = 3
        ring = sb("ring", [P, RING, HALF])

        stats = sb("stats", [P, T, 6])
        mean_var = sb("mean_var", [P, T, 2])
        rstd = sb("rstd", [P, T])
        shift = sb("shift", [P, T])
        minus_half = sb("minus_half", [P, T])
        s1_col = [sb(f"s1_col{k}", [P, T]) for k in SLOTS]
        top = [sb(f"top{k}", [P, T]) for k in SLOTS]
        top2 = [sb(f"top2{k}", [P, T]) for k in SLOTS]
        c_col = [sb(f"c_col{k}", [P, T]) for k in SLOTS]
        rsum = [sb(f"rsum{k}", [P, T]) for k in SLOTS]

        ident = sb("ident", [P, P])
        ident_b = sb("ident_b", [P, P], BF16)
        w0_1 = sb("w0_1", [P, D])
        w0_2 = sb("w0_2", [P, D])
        w2 = sb("w2", [P, D])
        w3 = sb("w3", [P, D])
        g0 = sb("g0", [P, D])
        v0_j = sb("v0_j", [P, 1])
        v_i = [sb(f"v_i{n}", [P, 1]) for n in range(3)]
        v_j = [sb(f"v_j{n}", [P, P]) for n in range(2)]
        const3 = sb("const3", [P, 1])
        bias3 = sb("bias3", [P, D])
        wg_in = sb("wg_in", [P, GRU_LAYERS, 3 * D])
        wg_h = sb("wg_h", [P, 3 * D])
        b_ih = sb("b_ih", [P, 3])
        b_hh = sb("b_hh", [P, 3])
        gate_bias = sb("gate_bias", [P, 4])

        psum = ctx.enter_context(nc.psum_tensor("psum", [P, 8, HALF], F32))

        ident_ready = steps("ident_ready")
        weights = steps("weights_ready")
        setup_pe = steps("setup_products")
        loaded_w = sem("loaded_w")
        x_in = [sem(f"x_in{k}") for k in SLOTS]
        adj_loaded = [[sem(f"adj_loaded{k}_{c}") for c in range(CHUNKS)] for k in SLOTS]
        go = sem("next_pass")
        arrived = sem("engines_arrived")
        pe_s = steps("pe_step")
        act_s = steps("act_step")
        dve_s = steps("dve_step")
        pool_s = steps("pool_step")
        stored = sem("stored")
        per_pass = [arrived, pe_s.sem, act_s.sem, dve_s.sem, pool_s.sem, stored]
        assert [s.num for s in per_pass] == list(range(arrived.num, arrived.num + len(per_pass)))

        setup_at = [base + edge_bytes]

        def raw_tile(name, shape):
            tile = nc.alloc_sbuf_tensor_at(name, shape, F32, offset=setup_at[0])
            setup_at[0] += 4 * int(np.prod(shape[1:]))
            setup_at[0] = (setup_at[0] + 31) // 32 * 32
            return tile

        raw = {n: raw_tile(f"raw_{n}", s) for n, s in {
            "W0": [P, D], "W0T": [P, D], "a_12": [P, D], "a12WT": [P, D], "W2T": [P, D], "W3": [P, D],
            "w_ih": [P, 3, D], "w_ihT": [P, 3 * D], "w_hh": [P, 3, D], "weight": [P, GRU_LAYERS, D], "weightT": [P, GRU_LAYERS, D],
            "a_1": [P, 1], "a_2": [P, 1], "a2": [P, 2], "ai_w": [P, 1], "aj_w": [P, 1], "aij": [P, 1],
            "W_b": [P, 1], "b_rep": [P, D], "aib": [P, 1], "ajb": [P, 1]}.items()}

        def column(ap):
            return ap.rearrange("(p o) -> p o", o=1)

        def everywhere(ap, n):
            return ap.rearrange("(o n) -> o n", o=1).broadcast_to([P, n])

        loads = [
            (raw["W0"][:], p0["W"]), (w2[:], p2["W"]), (raw["W3"][:], p3["W_w"]), (raw["a_12"][:], p0["a_12"]),
            (raw["w_hh"][:], p1["w_hh"].rearrange("(g p) d -> p g d", p=P)), (raw["w_ih"][:], p1["w_ih"].rearrange("(g p) d -> p g d", p=P)),
            (raw["weight"][:], p1["weight"].rearrange("l d e -> d l e")),
            (w0_1[:], p0["W_1"]), (w0_2[:], p0["W_2"]),
            (raw["a_1"][:], p0["a_1"]), (raw["a_2"][:], p0["a_2"]), 
            (raw["ai_w"][:], p3["ai_w"].rearrange("o p -> p o")), (raw["aj_w"][:], p3["aj_w"].rearrange("o p -> p o")),
            (raw["W_b"][:], column(p3["W_b"])), (bias3[:], everywhere(p3["W_b"], D)),
            (raw["aib"][:], everywhere(p3["ai_b"], 1)), (raw["ajb"][:], everywhere(p3["aj_b"], 1)),
        ]
        loads += [(raw["a2"][:, c:c + 1], p2["a"][c * P:(c + 1) * P, :]) for c in range(2)]
        for g in range(3):
            loads += [(b_ih[:, g:g + 1], column(p1["b_ih"][g * D:(g + 1) * D])), (b_hh[:, g:g + 1], column(p1["b_hh"][g * D:(g + 1) * D]))]
        N_LOADS = len(loads)
        plan = [("norm", 0, "att0"), ("norm", 1, "att0")]
        plan += [("prep", 0, "att0"), ("prep", 1, "att0"), ("top", 0, "att0"), ("top", 1, "att0")]
        plan += [("mix", 0, "att0"), ("mix", 1, "att0")]
        plan += [("norm", 0, "gru"), ("norm", 1, "gru")]
        for l in range(GRU_LAYERS):
            plan += [("gather", 0, l), ("back", 1, l - 1), ("gates", 0, l), ("gather", 1, l), ("back", 0, l), ("gates", 1, l)]
        plan += [("back", 1, GRU_LAYERS - 1)]
        plan = [s for s in plan if not (s[0] == "back" and s[2] < 0)]
        for L in ("att2", "att3"):
            for k in SLOTS:
                plan += [("norm", k, L), ("prep", k, L), ("top", k, L)]
            plan += [("mix", 0, L), ("mix", 1, L)]

        def bank(b):
            return psum[:, b, :]

        def tile_of(ap, t):
            return ap[:, t * P:(t + 1) * P]

        def half_of(ap, h):
            return ap[:, h * HALF:(h + 1) * HALF]

        def acc(t):
            return psum[:, t // 3, (t % 3) * VW:(t % 3 + 1) * VW]

        Y_BANKS = (6, 7, 3)
        h_flat = h_nat[:].rearrange("p t d -> p (t d)")
        unkept = [h_flat.bitcast(BF16)[:, n * N:(n + 1) * N] for n in range(2)]
        gru_scratch = [[half_of(vals[0], 0), half_of(vals[0], 1), half_of(h_flat, 0), half_of(h_flat, 1)],
                       [half_of(vals[1], 0), half_of(vals[1], 1), ring[:, 0, :], ring[:, 1, :]]]
        UNITS = [(t, h) for h in range(H) for t in range(T)]

        norms = [(k, L) for stage, k, L in plan if stage == "norm"]
        previous = dict(zip(norms[1:], norms))

        block = ctx.enter_context(nc.Block())

        @block.tensor
        def _(pe):
            pe.wait_ge(*ident_ready.at("ident"))
            pe.wait_ge(loaded_w, 16 * N_LOADS)
            def tr(b, src):
                return pe.transpose(bank(b)[:, 0:P], src, ident[:])

            tr(0, raw["W0"][:]).then_inc(*setup_pe.done("W0T"))
            tr(1, raw["W3"][:]).then_inc(*setup_pe.done("W3"))
            tr(2, w2[:]).then_inc(*setup_pe.done("W2T"))
            for g in range(3):
                tr(3 + g, raw["w_hh"][:, g, :]).then_inc(*setup_pe.done("w_hh", g))
            pe.wait_ge(*weights.at("copies1"))
            for g in range(3):
                tr(3 + g, raw["w_ih"][:, g, :]).then_inc(*setup_pe.done("w_ih", g))
            for l in range(GRU_LAYERS):
                tr(l, raw["weight"][:, l, :]).then_inc(*setup_pe.done("weight", l))
            pe.wait_ge(*weights.at("copies2"))
            for l in range(GRU_LAYERS):
                pe.matmul(bank(l)[:, 0:3 * D], raw["weightT"][:, l, :], raw["w_ihT"][:], start=True, stop=True).then_inc(*setup_pe.done("wg_in", l))
            pe.matmul(bank(3)[:, 0:P], raw["a_12"][:], raw["W0T"][:], start=True, stop=True).then_inc(*setup_pe.done("a12W"))
            pe.matmul(bank(4)[:, 0:1], raw["W0T"][:], raw["a_1"][:], start=True, stop=True)
            pe.matmul(bank(4)[:, 1:2], raw["W0T"][:], raw["a_2"][:], start=True, stop=True)
            pe.matmul(bank(4)[:, 2:3], raw["W2T"][:], raw["a2"][:, 0:1], start=True, stop=True)
            pe.matmul(bank(4)[:, 3:4], raw["W2T"][:], raw["a2"][:, 1:2], start=True, stop=True)
            pe.matmul(bank(4)[:, 4:5], raw["W3"][:], raw["ai_w"][:], start=True, stop=True)
            pe.matmul(bank(4)[:, 5:6], raw["W3"][:], raw["aj_w"][:], start=True, stop=True)
            pe.matmul(bank(4)[:, 6:7], raw["b_rep"][:], raw["aij"][:], start=True, stop=True).then_inc(*setup_pe.done("vectors"))
            pe.wait_ge(*weights.at("copies3"))
            pe.matmul(bank(5)[:, 0:P], raw["a12WT"][:], raw["W0T"][:], start=True, stop=True).then_inc(*setup_pe.done("g0"))
            pe.wait_ge(*weights.at("all"))

            with pe.Fori(0, PAIRS) as pair:
                busy = {}

                def take(*banks):
                    for b in banks:
                        if b in busy:
                            pe.wait_ge(*busy.pop(b))

                def norm(k, L):
                    for h in range(H):
                        take(6 + h)
                        for t in range(h * TH, (h + 1) * TH):
                            pe.wait_ge(*act_s.at("h_nat", k, L, t))
                            m = pe.transpose(tile_of(bank(6 + h), t - h * TH), h_nat[:, t, :], ident[:])
                        m.then_inc(*pe_s.done("hT", k, L, h))
                        busy[6 + h] = act_s.at("hT", k, L, h)

                def prep(k, L):
                    n = {"att0": 0, "att2": 1, "att3": 2}[L]
                    w_val = {"att0": w0_2, "att2": w2, "att3": w3}[L]
                    for h in range(H):
                        pe.wait_ge(*act_s.at("hT", k, L, h))
                    if L == "att0":
                        for h in range(H):
                            take(4 + h)
                            pe.matmul(bank(4 + h), g0[:], half_of(hT[k], h), start=True, stop=True).then_inc(*pe_s.done("q", k, h))
                            busy[4 + h] = dve_s.at("q_lo", k, h)
                    for h in range(H):
                        take(6 + h)
                        for t in range(h * TH, (h + 1) * TH):
                            m = pe.matmul(tile_of(bank(6 + h), t - h * TH), tile_of(hT[k], t), w_val[:], start=True, stop=True)
                        m.then_inc(*pe_s.done("vals", k, L, h))
                        busy[6 + h] = dve_s.at("vals", k, L, h)
                    if L == "att0":
                        for h in range(H):
                            take(h)
                            for t in range(h * TH, (h + 1) * TH):
                                m = pe.matmul(tile_of(bank(h), t - h * TH), tile_of(hT[k], t), w0_1[:], start=True, stop=True)
                            m.then_inc(*pe_s.done("extra", k, h))
                            busy[h] = act_s.at("extra", k, h)
                    take(4)
                    for t in range(T):
                        m = pe.matmul(psum[:, 4, t:t + 1], tile_of(hT[k], t), v_i[n][:], start=True, stop=True)
                    m.then_inc(*pe_s.done("s1_col", k, L))
                    busy[4] = dve_s.at("s1_col", k, L)
                    if L != "att2":
                        for h in range(H):
                            b = 5 - h
                            take(b)
                            pe.matmul(psum[0:1, b, :], v_i[n][:], half_of(hT[k], h), start=True, stop=True).then_inc(*pe_s.done("s1_row", k, L, h))
                            busy[b] = dve_s.at("s1_row", k, L, h)

                def top_(k, L):
                    if L == "att0":
                        for h in range(H):
                            pe.wait_ge(*dve_s.at("q_lo", k, h))
                            pe.wait_ge(*dve_s.at("hT_lo", k, h))
                        for t in range(T):
                            b = 2 * (t % 2)
                            take(b, b + 1)
                            for h in range(H):
                                pe.matmul(bank(b + h), tile_of(part_hi[k], t), half_of(hT_hi[k], h), start=True, stop=False)
                                pe.matmul(bank(b + h), tile_of(part_hi[k], t), half_of(hT_lo[k], h), start=False, stop=False)
                                m = pe.matmul(bank(b + h), tile_of(part_lo[k], t), half_of(hT_hi[k], h), start=False, stop=True)
                            m.then_inc(*pe_s.done("qh", k, t))
                            busy[b] = busy[b + 1] = dve_s.at("top", k, L, t)
                    else:
                        n = {"att2": 0, "att3": 1}[L]
                        b = 2 * k
                        take(b, b + 1)
                        for h in range(H):
                            m = pe.matmul(bank(b + h), v_j[n][:], half_of(hT[k], h), start=True, stop=True)
                        m.then_inc(*pe_s.done("s2", k, L))
                        busy[b] = busy[b + 1] = dve_s.at("top", k, L, T - 1)
                    pe.wait_ge(*dve_s.at("c_col", k, L))
                    for h in range(H):
                        take(4 + h)
                        for t in range(h * TH, (h + 1) * TH):
                            m = pe.matmul(psum[0:1, 4 + h, (t - h * TH) * P:(t - h * TH + 1) * P], c_col[k][:, t:t + 1], ident[:], start=True, stop=True)
                        m.then_inc(*pe_s.done("c_row", k, L, h))
                        busy[4 + h] = dve_s.at("c_row", k, L, h)

                def mix(k, L):
                    for h in range(H):
                        pe.wait_ge(*dve_s.at("c_row", k, L, h))
                        if L != "att2":
                            pe.wait_ge(*dve_s.at("s1_row", k, L, h))
                        if L != "att0":
                            pe.wait_ge(*dve_s.at("s2_row", k, L, h))
                        pe.wait_ge(*dve_s.at("vals", k, L, h))
                    rows = 2 * 32 if L == "att0" else P

                    def logits(u):
                        t, h = UNITS[u]
                        b = Y_BANKS[u % 3]
                        take(b)
                        for i in range(TH):
                            pe.matmul(tile_of(bank(b), i), tile_of(mask[k][:, h * TH + i, :], t), ident_b[:],
                                      start=i == 0, stop=False, skip_group_check=True)
                        if L == "att0":
                            for one, other in ((hT_hi, part_hi), (hT_lo, part_hi), (hT_hi, part_lo)):
                                pe.matmul(bank(b), tile_of(one[k], t), half_of(other[k], h), start=False, stop=False, skip_group_check=True)
                        m = pe.matmul(bank(b), tile_of(rows_j[k][0:rows, :], t), half_of(rows_i[k][0:rows, :], h), start=False, stop=True, skip_group_check=True)
                        m.then_inc(*pe_s.done("logits", k, L, u))
                        busy[b] = act_s.at("probs", k, L, u) if L == "att2" else dve_s.at("leaky", k, L, u)

                    def less_top(u):
                        t, h = UNITS[u]
                        pe.wait_ge(*act_s.at("relu", k, L, u))
                        pe.matmul(bank(Y_BANKS[u % 3]), tile_of(rows_j[k][0:64, :], t), half_of(rows_c[k], h), start=False, stop=True,
                                  skip_group_check=True).then_inc(*pe_s.done("less_top", k, L, u))

                    def weigh(u):
                        t, h = UNITS[u]
                        pe.wait_ge(*act_s.at("probs", k, L, u))
                        if u == 0:
                            take(0, 1, 2)
                        for i in range(TH):
                            o = h * TH + i
                            m = pe.matmul(acc(o), tile_of(ring[:, u % RING, :], i), vals[k][:, t * VW:(t + 1) * VW],
                                          start=t == 0 and (o % 3 == 0), stop=t == T - 1, skip_group_check=True)
                        m.then_inc(*pe_s.done("weighed", k, L, u))

                    LAG = 2
                    for u in range(len(UNITS) + LAG):
                        if u < len(UNITS):
                            logits(u)
                        if L != "att2" and 1 <= u <= len(UNITS):
                            less_top(u - 1)
                        if u >= LAG:
                            weigh(u - LAG)
                    for b in range(3):
                        busy[b] = dve_s.at("mixed", k, L)

                def gather(k, l):
                    for h in range(H):
                        if l == 0 and h == 0:
                            for t in range(T):
                                pe.wait_ge(*dve_s.at("edges", k, t))
                        take(h)
                        for t in range(T):
                            if h == 0:
                                hh = t // TH
                                if l == 0:
                                    pe.wait_ge(*dve_s.at("state_lo", k))
                                elif t % TH == 0:
                                    pe.wait_ge(*dve_s.at("nat_lo", k, l - 1, hh))
                            for part in (part_hi, part_lo):
                                m = pe.matmul(bank(h), tile_of(part[k], t), edges[k][:, t, h * HALF:(h + 1) * HALF],
                                              start=t == 0 and part is part_hi, stop=t == T - 1 and part is part_lo)
                        m.then_inc(*pe_s.done("sum", k, l, h))
                        busy[h] = act_s.at("sum", k, l, h)

                def gates(k, l):
                    state = hT[k]
                    for h in range(H):
                        if l == 0:
                            pe.wait_ge(*act_s.at("hT", k, "gru", h))
                        else:
                            pe.wait_ge(*dve_s.at("state", k, l - 1, h))
                        pe.wait_ge(*act_s.at("sum", k, l, h))
                        inp, hid = half_of(extra[k], h), half_of(state, h)
                        for g in range(2):
                            take(4 + g)
                            pe.matmul(bank(4 + g), wg_h[:, g * D:(g + 1) * D], hid, start=True, stop=False)
                            pe.matmul(bank(4 + g), wg_in[:, l, g * D:(g + 1) * D], inp, start=False, stop=True).then_inc(*pe_s.done("gate", k, l, h, g))
                            busy[4 + g] = act_s.at("gate", k, l, h, g)
                        take(6)
                        pe.matmul(bank(6), wg_h[:, 2 * D:3 * D], hid, start=True, stop=True).then_inc(*pe_s.done("gate", k, l, h, 2))
                        busy[6] = act_s.at("gate", k, l, h, 2)
                        take(7)
                        pe.matmul(bank(7), wg_in[:, l, 2 * D:3 * D], inp, start=True, stop=True).then_inc(*pe_s.done("gate", k, l, h, 3))
                        busy[7] = dve_s.at("n_sum", k, l, h)

                def back(k, l):
                    for h in range(H):
                        pe.wait_ge(*dve_s.at("state", k, l, h))
                        take(2 + h)
                        for i in range(TH):
                            m = pe.transpose(tile_of(bank(2 + h), i), tile_of(half_of(hT[k], h), i), ident[:])
                        m.then_inc(*pe_s.done("nat", k, l, h))
                        busy[2 + h] = dve_s.at("nat_lo", k, l, h) if l < GRU_LAYERS - 1 else dve_s.at("x_gru", k, h)

                for stage, k, what in plan:
                    {"norm": norm, "prep": prep, "top": top_, "mix": mix, "gather": gather, "gates": gates, "back": back}[stage](k, what)
                pe.drain().then_inc(arrived, 1)
                pe.wait_ge(go, pair + 1)

        @block.scalar
        def _(act):
            with act.Fori(0, PAIRS) as pair:

                def norm(k, L):
                    act.wait_ge(*dve_s.at("shift", k, L))
                    act.wait_ge(*pool_s.at("rstd", k, L))
                    if (k, L) in previous:
                        pk, pL = previous[(k, L)]
                        act.wait_ge(*pe_s.at("hT", pk, pL, H - 1))
                        if pL == "gru":
                            act.wait_ge(*dve_s.at("state_lo", pk))
                    for t in range(T):
                        act.activation(h_nat[:, t, :], xs[k][:, t, :], ACT.Relu, bias=shift[:, t:t + 1], scale=rstd[:, t:t + 1]).then_inc(*act_s.done("h_nat", k, L, t))
                    if L == "gru":
                        act.wait_ge(*act_s.last())
                        act.activation(part_hi[k][:], h_nat[:].rearrange("p t d -> p (t d)"), ACT.Copy).then_inc(*act_s.done("state_hi", k))
                    for h in range(H):
                        act.wait_ge(*pe_s.at("hT", k, L, h))
                        act.activation(half_of(hT[k], h), bank(6 + h), ACT.Copy).then_inc(*act_s.done("hT", k, L, h))

                def prep(k, L):
                    if L == "att0":
                        for h in range(H):
                            act.wait_ge(*act_s.at("hT", k, L, h))
                            act.activation(half_of(hT_hi[k], h), half_of(hT[k], h), ACT.Copy).then_inc(*act_s.done("hT_hi", k, h))
                        for h in range(H):
                            act.wait_ge(*pe_s.at("q", k, h))
                            act.activation(half_of(part_hi[k], h), bank(4 + h), ACT.Identity, bias=v0_j[:, 0:1]).then_inc(*act_s.done("q_hi", k, h))
                        for h in range(H):
                            act.wait_ge(*pe_s.at("extra", k, h))
                            act.activation(half_of(extra[k], h), bank(h), ACT.Copy).then_inc(*act_s.done("extra", k, h))
                    if L != "att2":
                        for h in range(H):
                            act.wait_ge(*pe_s.at("s1_row", k, L, h))
                            act.activation(half_of(rows_i[k][0:1, :], h), psum[0:1, 5 - h, :], ACT.Identity,
                                           bias=const3[0:1, 0:1] if L == "att3" else 0.0).then_inc(*act_s.done("s1_row", k, L, h))

                def top_(k, L):
                    if L != "att0":
                        act.wait_ge(*pe_s.at("s2", k, L))
                        for h in range(H):
                            act.activation(half_of(rows_j[k][64:65, :], h), psum[0:1, 2 * k + h, :], ACT.Copy).then_inc(*act_s.done("s2_row", k, L, h))
                    dst = rows_i if L == "att2" else rows_c
                    for h in range(H):
                        act.wait_ge(*pe_s.at("c_row", k, L, h))
                        act.activation(half_of(dst[k][0:1, :], h), psum[0:1, 4 + h, :], ACT.Copy).then_inc(*act_s.done("c_row", k, L, h))

                def mix(k, L):
                    n = len(UNITS)

                    def relu(u):
                        act.wait_ge(*pe_s.at("logits", k, L, u))
                        if u >= RING:
                            act.wait_ge(*pe_s.at("weighed", k, L, u - RING))
                        act.activation(ring[:, u % RING, :], bank(Y_BANKS[u % 3]), ACT.Relu, scale=STEEP).then_inc(*act_s.done("relu", k, L, u))

                    def probs(u):
                        if L == "att2":
                            act.wait_ge(*pe_s.at("logits", k, L, u))
                            if u >= RING:
                                act.wait_ge(*pe_s.at("weighed", k, L, u - RING))
                            act.activation(ring[:, u % RING, :], bank(Y_BANKS[u % 3]), ACT.Exp).then_inc(*act_s.done("probs", k, L, u))
                        else:
                            act.wait_ge(*dve_s.at("leaky", k, L, u))
                            act.activation(ring[:, u % RING, :], ring[:, u % RING, :], ACT.Exp, scale=ALPHA).then_inc(*act_s.done("probs", k, L, u))

                    if L == "att2":
                        for u in range(n):
                            probs(u)
                    else:
                        for u in range(n + 1):
                            if u < n:
                                relu(u)
                            if u >= 1:
                                probs(u - 1)
                    act.wait_ge(*dve_s.at("mixed", k, L))
                    act.activation(hT[k][:], vals[k][:, 0:N], ACT.Relu, scale=-1.0).then_inc(*act_s.done("below", k, L))
                    act.wait_ge(*act_s.last())
                    act.activation(hT[k][:], hT[k][:], ACT.Exp, scale=-1.0).then_inc(*act_s.done("elu_exp", k, L))

                def gather(k, l):
                    for h in range(H):
                        act.wait_ge(*pe_s.at("sum", k, l, h))
                        act.activation(half_of(extra[k], h), bank(h), ACT.Copy).then_inc(*act_s.done("sum", k, l, h))

                def gates(k, l):
                    r, z, hn, n = gru_scratch[k]
                    if l == 0 and k == 0:
                        act.wait_ge(*dve_s.at("state_lo", 1))
                    for h in range(H):
                        act.wait_ge(*pe_s.at("gate", k, l, h, 0))
                        if h > 0 or l > 0:
                            act.wait_ge(*dve_s.at("state", k, *((l, h - 1) if h else (l - 1, H - 1))))
                        act.activation(r, bank(4), ACT.Tanh, bias=gate_bias[:, 0:1], scale=0.5).then_inc(*act_s.done("gate", k, l, h, 0))
                        act.wait_ge(*pe_s.at("gate", k, l, h, 1))
                        act.activation(z, bank(5), ACT.Tanh, bias=gate_bias[:, 1:2], scale=0.5).then_inc(*act_s.done("gate", k, l, h, 1))
                        act.wait_ge(*pe_s.at("gate", k, l, h, 2))
                        act.activation(hn, bank(6), ACT.Identity, bias=gate_bias[:, 2:3], scale=0.5).then_inc(*act_s.done("gate", k, l, h, 2))
                        act.wait_ge(*dve_s.at("n_sum", k, l, h))
                        act.activation(n, hn, ACT.Tanh, bias=gate_bias[:, 3:4]).then_inc(*act_s.done("n", k, l, h))

                def back(k, l):
                    if l < GRU_LAYERS - 1:
                        for h in range(H):
                            act.wait_ge(*pe_s.at("nat", k, l, h))
                            act.activation(half_of(part_hi[k], h), bank(2 + h), ACT.Copy).then_inc(*act_s.done("nat_hi", k, l, h))

                for stage, k, what in plan:
                    {"norm": norm, "prep": prep, "top": top_, "mix": mix, "gather": gather, "gates": gates, "back": back}[stage](k, what)
                act.drain().then_inc(arrived, 1)
                act.wait_ge(go, pair + 1)

        @block.vector
        def _(dve):
            def copy_w(dst, src, step, label=None):
                dve.wait_ge(*setup_pe.at(*step))
                dve.tensor_copy(dst, src).then_inc(*weights.done(*(label or ("copied",) + step)))

            dve.wait_ge(loaded_w, 16 * N_LOADS)
            dve.wait_ge(*ident_ready.at("ident"))
            dve.tensor_copy(ident_b[:], ident[:]).then_inc(*weights.done("ident_b"))
            dve.tensor_copy(raw["b_rep"][:], raw["W_b"][:].broadcast_to([P, P])).then_inc(*weights.done("b_rep"))
            dve.tensor_tensor(raw["aij"][:], raw["ai_w"][:], raw["aj_w"][:], ALU.add).then_inc(*weights.done("aij"))
            for g in range(2):
                dve.tensor_scalar(gate_bias[:, g:g + 1], b_ih[:, g:g + 1], b_hh[:, g:g + 1], 0.5, ALU.add, ALU.mult).then_inc(*weights.done("gate_bias", g))
            dve.tensor_scalar(gate_bias[:, 2:3], b_hh[:, 2:3], 0.5, None, ALU.mult).then_inc(*weights.done("gate_bias", 2))
            dve.tensor_copy(gate_bias[:, 3:4], b_ih[:, 2:3]).then_inc(*weights.done("gate_bias", 3))
            copy_w(raw["W0T"][:], bank(0)[:, 0:P], ("W0T",))
            copy_w(w3[:], bank(1)[:, 0:P], ("W3",))
            copy_w(raw["W2T"][:], bank(2)[:, 0:P], ("W2T",))
            for g in range(3):
                copy_w(wg_h[:, g * D:(g + 1) * D], bank(3 + g)[:, 0:P], ("w_hh", g), ("copies1",))
            for g in range(3):
                copy_w(raw["w_ihT"][:, g * D:(g + 1) * D], bank(3 + g)[:, 0:P], ("w_ih", g))
            for l in range(GRU_LAYERS):
                copy_w(raw["weightT"][:, l, :], bank(l)[:, 0:P], ("weight", l), ("copies2",))
            for l in range(GRU_LAYERS):
                copy_w(wg_in[:, l, :], bank(l)[:, 0:3 * D], ("wg_in", l))
            copy_w(raw["a12WT"][:], bank(3)[:, 0:P], ("a12W",), ("copies3",))
            copy_w(v0_j[:], psum[:, 4, 0:1], ("vectors",))
            for n, c in enumerate((1, 2, 4)):
                copy_w(v_i[n][:], psum[:, 4, c:c + 1], ("vectors",), ("v_i", n))
            for n, c in enumerate((3, 5)):
                copy_w(v_j[n][:], psum[:, 4, c:c + 1].broadcast_to([P, P]), ("vectors",), ("v_j", n))
            dve.tensor_scalar(const3[:], psum[:, 4, 6:7], raw["aib"][:, 0:1], raw["ajb"][:, 0:1], ALU.add, ALU.add).then_inc(*weights.done("const3"))
            copy_w(g0[:], bank(5)[:, 0:P], ("g0",))
            for k in SLOTS:
                dve.memset(rows_j[k][:].bitcast(F32), 0.0).then_inc(*weights.done("rows0", k))
                dve.memset(rows_i[k][:].bitcast(F32), 0.0).then_inc(*weights.done("rows0", k))
                dve.memset(rows_c[k][:].bitcast(F32), 0.0).then_inc(*weights.done("rows0", k))
            dve.wait_ge(*weights.last())
            for k in SLOTS:
                for p in (0, 32):
                    dve.memset(rows_j[k][p:p + 1, :].bitcast(F32), 1.0).then_inc(*weights.done("rows1", k, p))
                for p in (64, 96):
                    dve.memset(rows_i[k][p:p + 1, :].bitcast(F32), 1.0).then_inc(*weights.done("rows1", k, p))
            dve.engine_nop().then_inc(*weights.done("all"))
            dve.wait_ge(*weights.last())

            with dve.Fori(0, PAIRS) as pair:

                def norm(k, L):
                    if L == "att0":
                        dve.wait_ge(x_in[k], 16 * (pair + 1))
                    else:
                        dve.wait_ge(*dve_s.last())
                    if (k, L) in previous:
                        pk, pL = previous[(k, L)]
                        dve.wait_ge(*act_s.at("h_nat", pk, pL, T - 1))
                    for t in range(T):
                        m = dve.bn_stats(stats[:, t, :], xs[k][:, t, :])
                    m.then_inc(*dve_s.done("stats", k, L))
                    dve.wait_ge(*dve_s.last())
                    for t in range(T):
                        m = dve.bn_aggr(mean_var[:, t, :], stats[:, t, :])
                    m.then_inc(*dve_s.done("mean_var", k, L))
                    dve.wait_ge(*pool_s.at("rstd", k, L))
                    dve.scalar_tensor_tensor(shift[:], mean_var[:, :, 0], -1.0, rstd[:], ALU.mult, ALU.mult).then_inc(*dve_s.done("shift", k, L))
                    if L == "att0":
                        for t in range(T):
                            if t % CHUNK == 0:
                                dve.wait_ge(adj_loaded[k][t // CHUNK], 16 * (pair + 1))
                            dve.tensor_scalar(mask[k][:, t, :], adj_in[k][:, t, :], 0, MASKED, ALU.is_le, ALU.mult).then_inc(*dve_s.done("mask", k, t))
                    if L == "gru":
                        dve.wait_ge(*act_s.at("state_hi", k))
                        dve.tensor_tensor(part_lo[k][:], h_nat[:].rearrange("p t d -> p (t d)"), part_hi[k][:].bitcast(F32), ALU.subtract).then_inc(*dve_s.done("state_lo", k))

                def prep(k, L):
                    if L == "att0":
                        for h in range(H):
                            dve.wait_ge(*act_s.at("hT_hi", k, h))
                            dve.tensor_tensor(half_of(hT_lo[k], h), half_of(hT[k], h), half_of(hT_hi[k], h).bitcast(F32), ALU.subtract).then_inc(*dve_s.done("hT_lo", k, h))
                        for h in range(H):
                            dve.wait_ge(*act_s.at("q_hi", k, h))
                            dve.scalar_tensor_tensor(half_of(part_lo[k], h), bank(4 + h), v0_j[:, 0:1], half_of(part_hi[k], h).bitcast(F32), ALU.add, ALU.subtract).then_inc(*dve_s.done("q_lo", k, h))
                    v = vals[k][:].rearrange("p (t w) -> p t w", w=VW)
                    dve.memset(v[:, :, D:VW], 1.0).then_inc(*dve_s.done("ones", k, L))
                    for h in range(H):
                        dve.wait_ge(*pe_s.at("vals", k, L, h))
                        dst = v[:, h * TH:(h + 1) * TH, 0:D]
                        src = bank(6 + h).rearrange("p (t d) -> p t d", d=D)
                        if L == "att3":
                            dve.tensor_tensor(dst, src, bias3[:].rearrange("p (o d) -> p o d", o=1).broadcast_to([P, TH, D]), ALU.add).then_inc(*dve_s.done("vals", k, L, h))
                        else:
                            dve.tensor_copy(dst, src).then_inc(*dve_s.done("vals", k, L, h))
                    dve.wait_ge(*pe_s.at("s1_col", k, L))
                    if L == "att3":
                        dve.tensor_scalar(s1_col[k][:], psum[:, 4, 0:T], const3[:, 0:1], None, ALU.add).then_inc(*dve_s.done("s1_col", k, L))
                    else:
                        dve.tensor_copy(s1_col[k][:], psum[:, 4, 0:T]).then_inc(*dve_s.done("s1_col", k, L))
                    if L != "att2":
                        for h in range(H):
                            dve.wait_ge(*act_s.at("s1_row", k, L, h))
                            hi = half_of(rows_i[k][0:1, :], h).bitcast(F32)
                            src, lo = psum[0:1, 5 - h, :], half_of(rows_i[k][32:33, :], h)
                            if L == "att3":
                                dve.scalar_tensor_tensor(lo, src, const3[0:1, 0:1], hi, ALU.add, ALU.subtract).then_inc(*dve_s.done("s1_row", k, L, h))
                            else:
                                dve.tensor_tensor(lo, src, hi, ALU.subtract).then_inc(*dve_s.done("s1_row", k, L, h))

                def top_(k, L):
                    for t in range(T):
                        if L == "att0":
                            b = 2 * (t % 2)
                            dve.wait_ge(*pe_s.at("qh", k, t))
                            dve.wait_ge(*dve_s.at("mask", k, t))
                        else:
                            b = 2 * k
                            dve.wait_ge(*act_s.at("s2_row", k, L, H - 1))
                        if t >= 2:
                            dve.wait_ge(*dve_s.at("top", k, L, t - 2))
                        dve.tensor_tensor_reduce(unkept[t % 2], psum[:, b:b + 2, :].rearrange("p b n -> p (b n)"), mask[k][:, t, :], 1.0, LOWEST, ALU.add, ALU.max, top[k][:, t:t + 1]).then_inc(*dve_s.done("top", k, L, t))
                    if L != "att0":
                        for h in range(H):
                            dve.wait_ge(*act_s.at("s2_row", k, L, h))
                            dve.tensor_tensor(half_of(rows_j[k][96:97, :], h), psum[0:1, 2 * k + h, :], half_of(rows_j[k][64:65, :], h).bitcast(F32), ALU.subtract).then_inc(*dve_s.done("s2_row", k, L, h))
                    dve.wait_ge(*dve_s.at("top", k, L, T - 1))
                    dve.tensor_tensor(top[k][:], top[k][:], s1_col[k][:], ALU.add).then_inc(*dve_s.done("row_top", k, L))
                    dve.wait_ge(*dve_s.last())
                    if L == "att2":
                        dve.tensor_tensor(c_col[k][:], s1_col[k][:], top[k][:], ALU.subtract).then_inc(*dve_s.done("c_col", k, L))
                    else:
                        dve.tensor_scalar(top2[k][:], top[k][:], 0.0, -STEEP, ALU.max, ALU.mult).then_inc(*dve_s.done("top2", k, L))
                        dve.wait_ge(*dve_s.last())
                        dve.tensor_tensor(c_col[k][:], top2[k][:], top[k][:], ALU.subtract).then_inc(*dve_s.done("c_col", k, L))
                    dst = rows_i if L == "att2" else rows_c
                    for h in range(H):
                        dve.wait_ge(*act_s.at("c_row", k, L, h))
                        dve.tensor_tensor(half_of(dst[k][32:33, :], h), psum[0:1, 4 + h, :], half_of(dst[k][0:1, :], h).bitcast(F32), ALU.subtract).then_inc(*dve_s.done("c_row", k, L, h))

                def mix(k, L):
                    if L != "att2":
                        for u in range(len(UNITS)):
                            if L == "att0" and u % H == 0:
                                t = u // H
                                dve.tensor_scalar(edges[k][:, t, :], adj_in[k][:, t, :], 0, None, ALU.not_equal).then_inc(*dve_s.done("edges", k, t))
                            dve.wait_ge(*pe_s.at("less_top", k, L, u))
                            dve.tensor_tensor(ring[:, u % RING, :], bank(Y_BANKS[u % 3]), ring[:, u % RING, :], ALU.add).then_inc(*dve_s.done("leaky", k, L, u))
                    dve.wait_ge(*pe_s.at("weighed", k, L, len(UNITS) - 1))
                    for b in range(3):
                        n = min(3, T - 3 * b)
                        s = psum[:, b, 0:n * VW].rearrange("p (t w) -> p t w", w=VW)[:, :, D]
                        m = dve.reciprocal(rsum[k][:, 3 * b:3 * b + n], s)
                    m.then_inc(*dve_s.done("rsum", k, L))
                    dve.wait_ge(*dve_s.last())
                    for t in range(T):
                        dst = vals[k][:, t * D:(t + 1) * D]
                        if L == "att0":
                            m = dve.scalar_tensor_tensor(dst, acc(t)[:, 0:D], rsum[k][:, t:t + 1], tile_of(extra[k], t), ALU.mult, ALU.add)
                        else:
                            m = dve.tensor_scalar(dst, acc(t)[:, 0:D], rsum[k][:, t:t + 1], None, ALU.mult)
                    m.then_inc(*dve_s.done("mixed", k, L))
                    xk = xs[k][:].rearrange("p t d -> p (t d)")
                    dve.wait_ge(*act_s.at("elu_exp", k, L))
                    dve.scalar_tensor_tensor(xk, hT[k][:], -1.0, xk, ALU.add, ALU.add).then_inc(*dve_s.done("x_part", k, L))
                    dve.wait_ge(*dve_s.last())
                    dve.scalar_tensor_tensor(xk, vals[k][:, 0:N], 0.0, xk, ALU.max, ALU.add).then_inc(*dve_s.done("x", k, L))

                def gather(k, l):
                    pass

                def gates(k, l):
                    r, z, hn, n = gru_scratch[k]
                    for h in range(H):
                        dve.wait_ge(*act_s.at("gate", k, l, h, 2))
                        dve.scalar_tensor_tensor(hn, r, 1.0, hn, ALU.add, ALU.mult).then_inc(*dve_s.done("r_n", k, l, h))
                        dve.wait_ge(*pe_s.at("gate", k, l, h, 3))
                        dve.wait_ge(*dve_s.last())
                        dve.tensor_tensor(hn, bank(7), hn, ALU.add).then_inc(*dve_s.done("n_sum", k, l, h))
                        dve.wait_ge(*act_s.at("n", k, l, h))
                        dve.tensor_tensor(r, half_of(hT[k], h), n, ALU.subtract).then_inc(*dve_s.done("h_less_n", k, l, h))
                        dve.wait_ge(*dve_s.last())
                        dve.scalar_tensor_tensor(r, z, 1.0, r, ALU.add, ALU.mult).then_inc(*dve_s.done("z_part", k, l, h))
                        dve.wait_ge(*dve_s.last())
                        dve.scalar_tensor_tensor(half_of(hT[k], h), r, 0.5, n, ALU.mult, ALU.add).then_inc(*dve_s.done("state", k, l, h))

                def back(k, l):
                    for h in range(H):
                        if l < GRU_LAYERS - 1:
                            dve.wait_ge(*act_s.at("nat_hi", k, l, h))
                            dve.tensor_tensor(half_of(part_lo[k], h), bank(2 + h), half_of(part_hi[k], h).bitcast(F32), ALU.subtract).then_inc(*dve_s.done("nat_lo", k, l, h))
                        else:
                            dve.wait_ge(*pe_s.at("nat", k, l, h))
                            xk = half_of(xs[k][:].rearrange("p t d -> p (t d)"), h)
                            dve.tensor_tensor(xk, bank(2 + h), xk, ALU.add).then_inc(*dve_s.done("x_gru", k, h))

                for stage, k, what in plan:
                    {"norm": norm, "prep": prep, "top": top_, "mix": mix, "gather": gather, "gates": gates, "back": back}[stage](k, what)
                dve.drain().then_inc(arrived, 1)
                dve.wait_ge(go, pair + 1)

        @block.gpsimd
        def _(pool):
            pool.memset(minus_half[:], -0.5).then_inc(*ident_ready.done("half"))
            pool.memset(ident[:], 0.0).then_inc(*ident_ready.done("zero"))
            pool.wait_ge(*ident_ready.last())
            pool.affine_select(out=ident[:], in_=ident[:], compare_op=ALU.not_equal, fill=1.0, base=0,
                               pattern=[[-1, P]], channel_multiplier=1).then_inc(*ident_ready.done("ident"))
            with pool.Fori(0, PAIRS) as pair:
                for stage, k, L in plan:
                    if stage == "norm":
                        pool.wait_ge(*dve_s.at("mean_var", k, L))
                        pool.tensor_scalar(rstd[:], mean_var[:, :, 1], EPS, 1.0, ALU.add, ALU.mult).then_inc(*pool_s.done("var", k, L))
                        pool.wait_ge(*pool_s.last())
                        pool.tensor_tensor(rstd[:], rstd[:], minus_half[:], ALU.pow).then_inc(*pool_s.done("rstd", k, L))
                pool.drain().then_inc(arrived, 1)
                pool.wait_ge(go, pair + 1)

        @block.sync
        def _(sp):
            def load_x(k, pair):
                sp.dma_start(xs[k][:], x.rearrange("g (t p) d -> g p t d", p=P)[bass.ds(2 * pair + k, 1)].rearrange("o p t d -> (o p) t d")).then_inc(x_in[k], 16)

            def load_adj(k, pair):
                g = adj.rearrange("g (t p) n -> g p t n", p=P)[bass.ds(2 * pair + k, 1)].rearrange("o p t n -> (o p) t n")
                for c in range(CHUNKS):
                    sp.dma_start(adj_in[k][:, c * CHUNK:(c + 1) * CHUNK, :], g[:, c * CHUNK:(c + 1) * CHUNK, :]).then_inc(adj_loaded[k][c], 16)

            def store(k, pair):
                sp.wait_ge(*dve_s.at("x", k, "att3"))
                sp.dma_start(out.rearrange("g (t p) d -> g p t d", p=P)[bass.ds(2 * pair + k, 1)].rearrange("o p t d -> (o p) t d"), xs[k][:]).then_inc(stored, 16)

            for k in SLOTS:
                load_x(k, 0)
            for dst, src in loads:
                sp.dma_start(dst, src).then_inc(loaded_w, 16)
            load_adj(0, 0)
            sp.wait_ge(*weights.at("all"))
            load_adj(1, 0)

            def end_of_pass(pair):
                for k in SLOTS:
                    store(k, pair)
                sp.wait_ge(stored, 16 * len(SLOTS))
                sp.wait_ge(arrived, 4)
                sp.sem_clear(range(per_pass[0].num, per_pass[-1].num + 1))
                sp.sem_inc(go, 1)

            with sp.Fori(0, PAIRS - 1) as pair:
                for k in SLOTS:
                    sp.wait_ge(*pe_s.at("sum", k, GRU_LAYERS - 1, H - 1))
                    load_adj(k, pair + 1)
                end_of_pass(pair)
                for k in SLOTS:
                    load_x(k, pair + 1)
            end_of_pass(PAIRS - 1)


_ARGS = {
    "x": "x", "adj": "adj",
    "p0": {"W": "L0_gnn_W", "a_1": "L0_gnn_a_1", "a_2": "L0_gnn_a_2", "a_12": "L0_gnn_a_12", "W_1": "L0_gnn_W_1", "W_2": "L0_gnn_W_2"},
    "p1": {"weight": "L1_gnn_weight", "w_ih": "L1_gnn_w_ih", "w_hh": "L1_gnn_w_hh", "b_ih": "L1_gnn_b_ih", "b_hh": "L1_gnn_b_hh"},
    "p2": {"W": "L2_gnn_W", "a": "L2_gnn_a"},
    "p3": {"W_w": "L3_gnn_W_w", "W_b": "L3_gnn_W_b", "ai_w": "L3_gnn_ai_w", "ai_b": "L3_gnn_ai_b", "aj_w": "L3_gnn_aj_w", "aj_b": "L3_gnn_aj_b"},
}


def kernel(**inputs):
    import concourse.bacc as _bacc
    from concourse.bass_utils import run_bass_kernel_spmd as _run

    counts = {}
    for _ in range(2):
        nc = _bacc.Bacc("TRN2", target_bir_lowering=False, num_devices=1)
        arrays = {}

        def dram(name):
            a = np.ascontiguousarray(inputs[name])
            arrays[f"in_{name}"] = a
            return nc.dram_tensor(f"in_{name}", a.shape, mybir.dt.from_np(a.dtype), kind="ExternalInput").ap()

        args = {k: dram(v) if isinstance(v, str) else {n: dram(m) for n, m in v.items()} for k, v in _ARGS.items()}
        args["out"] = nc.dram_tensor("out_x", args["x"].shape, F32, kind="ExternalOutput").ap()
        build(nc, counts, **args)
    r = _run(nc, [arrays], core_ids=[0])
    return r.results[0]["out_x"]
```

```python
from contextlib import ExitStack

import numpy as np

import concourse.bass as bass
from concourse import mybir
from concourse.alu_op_type import AluOpType as ALU

ACT = mybir.ActivationFunctionType
F32 = mybir.dt.float32
F32R = mybir.dt.float32r
BF16 = mybir.dt.bfloat16
I32 = mybir.dt.int32

P = 128
HALF = 512
MASKED = -9.0e15
LOWEST = -3.0e38
EPS = 1e-5
ALPHA = 0.2
STEEP = (1.0 - ALPHA) / ALPHA


class Steps:

    def __init__(self, sem, counts):
        self.sem, self.counts, self.n = sem, counts, 0

    def done(self, *step):
        self.n += 1
        self.counts[step] = self.n
        return self.sem, 1

    def at(self, *step):
        return self.sem, self.counts.get(step, 1)

    def last(self):
        return self.sem, self.n


def build(nc, counts, x, adj, p0, p1, p2, p3, out):
    GRAPHS, N, D = x.shape
    T = N // P
    H = N // HALF
    TH = T // H
    PAIRS = GRAPHS // 2
    GRU_LAYERS = p1["weight"].shape[0]
    VW = D + 1
    CHUNK = 2
    CHUNKS = T // CHUNK
    SLOTS = range(2)
    assert D == P and GRAPHS % 2 == 0

    with ExitStack() as ctx:
        def sb(name, shape, dt=F32):
            return ctx.enter_context(nc.sbuf_tensor(name, shape, dt))

        def sem(name):
            return ctx.enter_context(nc.semaphore(name))

        def steps(name):
            return Steps(sem(name), counts.setdefault(name, {}))

        edge_bytes = T * N * 4
        base = (nc.sbuf_base + 31) // 32 * 32
        sb("edge_slab", [P, 2 * edge_bytes // 4 + 8], I32)
        adj_in = [nc.alloc_sbuf_tensor_at(f"adj_in{k}", [P, T, N], I32, offset=base + k * edge_bytes) for k in SLOTS]
        edges = [nc.alloc_sbuf_tensor_at(f"edges{k}", [P, T, N], F32R, offset=base + k * edge_bytes) for k in SLOTS]

        RING = 5
        ring = sb("ring", [P, RING, HALF])
        gru_r, gru_z, gru_hn, gru_n = (ring[:, i, :] for i in range(4))

        mask = [sb(f"mask{k}", [P, T, N], BF16) for k in SLOTS]
        xs = [sb(f"xs{k}", [P, T, D]) for k in SLOTS]
        extra = [sb(f"extra{k}", [P, N]) for k in SLOTS]
        hT_hi = [sb(f"hT_hi{k}", [P, N], F32R) for k in SLOTS]
        hT_lo = [sb(f"hT_lo{k}", [P, N], F32R) for k in SLOTS]
        part_hi = [sb(f"part_hi{k}", [P, N], F32R) for k in SLOTS]
        part_lo = [sb(f"part_lo{k}", [P, N], F32R) for k in SLOTS]
        sum_lo = [sb(f"sum_lo{k}", [P, N], F32R) for k in SLOTS]
        sum_hi, vals = [], []
        for k in SLOTS:
            at = (nc.sbuf_base + 31) // 32 * 32
            sb(f"vals_place{k}", [P, T * VW + 8])
            sum_hi.append(nc.alloc_sbuf_tensor_at(f"sum_hi{k}", [P, N], F32R, offset=at))
            vals.append(nc.alloc_sbuf_tensor_at(f"vals{k}", [P, T, VW], F32, offset=at))
        S1, S2, C = slice(0, 2), slice(32, 34), slice(64, 66)
        S_ROWS, ALL_ROWS = slice(0, 34), slice(0, 66)
        rows_i = [sb(f"rows_i{k}", [P, N], F32R) for k in SLOTS]
        rows_j = [sb(f"rows_j{k}", [P, N], F32R) for k in SLOTS]
        lo_row = sb("lo_row", [P, 1])
        at = (nc.sbuf_base + 31) // 32 * 32
        sb("h_place", [P, T * D + 8])
        h_nat = nc.alloc_sbuf_tensor_at("h_nat", [P, T, D], F32, offset=at)
        s_hi = nc.alloc_sbuf_tensor_at("s_hi", [P, N], F32R, offset=at)

        stats = sb("stats", [P, T, 6])
        mean_var = sb("mean_var", [P, T, 2])
        rstd = sb("rstd", [P, T])
        shift = sb("shift", [P, T])
        minus_half = sb("minus_half", [P, T])
        s_col = [sb(f"s_col{k}", [P, T]) for k in SLOTS]
        top = [sb(f"top{k}", [P, T]) for k in SLOTS]
        top2 = [sb(f"top2{k}", [P, T]) for k in SLOTS]
        c_col = [sb(f"c_col{k}", [P, T]) for k in SLOTS]
        rsum = [sb(f"rsum{k}", [P, T]) for k in SLOTS]
        c_cols = [sb(f"c_cols{k}", [P, T, 2], F32R) for k in SLOTS]

        ident_b = sb("ident_b", [P, P], BF16)
        ident = sb("ident", [P, P])

        def parts(name, shape):
            return sb(name + "_hi", shape, F32R), sb(name + "_lo", shape, F32R)

        w0_1, w0_2, w2, w3 = (sb(n, [P, D]) for n in ("w0_1", "w0_2", "w2", "w3"))
        bias3 = sb("bias3", [P, D])
        g0 = parts("g0", [P, D])
        v_s = sb("v_s", [P, 3, S2.stop])
        const3 = sb("const3", [P, 1])
        wg_in = parts("wg_in", [P, GRU_LAYERS, 3 * D])
        wg_h = parts("wg_h", [P, 3 * D])
        b_ih = sb("b_ih", [P, 3])
        b_hh = sb("b_hh", [P, 3])
        gate_bias = sb("gate_bias", [P, 4])

        psum = ctx.enter_context(nc.psum_tensor("psum", [P, 8, HALF], F32))

        ident_ready = steps("ident_ready")
        weights = steps("weights_ready")
        setup_pe = steps("setup_products")
        loaded_w = sem("loaded_w")
        x_in = [sem(f"x_in{k}") for k in SLOTS]
        adj_loaded = [[sem(f"adj_loaded{k}_{c}") for c in range(CHUNKS)] for k in SLOTS]
        go = sem("next_pass")
        arrived = sem("engines_arrived")
        pe_s = steps("pe_step")
        act_s = steps("act_step")
        dve_s = steps("dve_step")
        pool_s = steps("pool_step")
        stored = sem("stored")
        per_pass = [arrived, pe_s.sem, act_s.sem, dve_s.sem, pool_s.sem, stored]
        assert [s.num for s in per_pass] == list(range(arrived.num, arrived.num + len(per_pass)))

        setup_at = [base + edge_bytes]

        def raw_tile(name, shape):
            tile = nc.alloc_sbuf_tensor_at(name, shape, F32, offset=setup_at[0])
            setup_at[0] += (4 * int(np.prod(shape[1:])) + 31) // 32 * 32
            return tile

        raw = {n: raw_tile(f"raw_{n}", s) for n, s in {
            "W0": [P, D], "W0T": [P, D], "a_12": [P, D], "a12WT": [P, D], "W2": [P, D], "W2T": [P, D], "W3": [P, D],
            "w_ih": [P, 3, D], "w_ihT": [P, 3 * D], "w_hh": [P, 3, D], "weight": [P, GRU_LAYERS, D], "weightT": [P, GRU_LAYERS, D],
            "a_1": [P, 1], "a_2": [P, 1], "a2": [P, 2], "ai_w": [P, 1], "aj_w": [P, 1], "aij": [P, 1],
            "W_b": [P, 1], "b_rep": [P, D], "aib": [P, 1], "ajb": [P, 1]}.items()}

        def column(ap):
            return ap.rearrange("(p o) -> p o", o=1)

        def everywhere(ap, n):
            return ap.rearrange("(o n) -> o n", o=1).broadcast_to([P, n])

        loads = [
            (raw["W0"][:], p0["W"]), (raw["W2"][:], p2["W"]), (raw["W3"][:], p3["W_w"]), (raw["a_12"][:], p0["a_12"]),
            (raw["w_hh"][:], p1["w_hh"].rearrange("(g p) d -> p g d", p=P)), (raw["w_ih"][:], p1["w_ih"].rearrange("(g p) d -> p g d", p=P)),
            (raw["weight"][:], p1["weight"].rearrange("l d e -> d l e")),
            (w0_1[:], p0["W_1"]), (w0_2[:], p0["W_2"]),
            (raw["a_1"][:], p0["a_1"]), (raw["a_2"][:], p0["a_2"]),
            (raw["ai_w"][:], p3["ai_w"].rearrange("o p -> p o")), (raw["aj_w"][:], p3["aj_w"].rearrange("o p -> p o")),
            (raw["W_b"][:], column(p3["W_b"])), (bias3[:], everywhere(p3["W_b"], D)),
            (raw["aib"][:], everywhere(p3["ai_b"], 1)), (raw["ajb"][:], everywhere(p3["aj_b"], 1)),
        ]
        loads += [(raw["a2"][:, c:c + 1], p2["a"][c * P:(c + 1) * P, :]) for c in range(2)]
        for g in range(3):
            loads += [(b_ih[:, g:g + 1], column(p1["b_ih"][g * D:(g + 1) * D])), (b_hh[:, g:g + 1], column(p1["b_hh"][g * D:(g + 1) * D]))]
        N_LOADS = len(loads)

        UNITS = [(t, h) for h in range(H) for t in range(T)]
        NU = len(UNITS)
        Y_BANKS = (6, 7, 3)
        LAG = 3

        def chain_steps(prev, L, part=slice(None)):
            s = []
            if prev in ("att0", "att2", "att3"):
                s += ["mixed", "below", "elu_exp", "x"]
            if L is None:
                return s[part]
            s += ["stats", "rstd", "shift"] + [("h_nat", t) for t in range(0, T, 2)]
            for h in range(H):
                s += [("turn", h), ("turned", h)]
            if L in ("att0", "gru"):
                s += [("split", h) for h in range(H)]
            if L == "gru":
                return (s + ["part_hi", "part_lo"])[part]
            s += [("s", h) for h in range(H)] + [("s_out", h) for h in range(H)]
            for what in ("vals", "q", "extra") if L == "att0" else ("vals",):
                s += [(what, h) for h in range(H)] + [(what + "_out", h) for h in range(H)]
            s += ["s_col", "s_col_out"]
            if L != "att0":
                s += ["s2"]
            s += [("top", t) for t in range(T)] + ["c_col", "c_cols", "c_row", "c_row_out"]
            return s[part]

        MIX, GRU = [(4, 5)], [(2, 3)]
        plan = [(None, (0, None, "att0"), [(4, 5), (6, 7)]),
                (("mix", 0, "att0"), (1, None, "att0"), MIX),
                (("mix", 1, "att0"), (0, "att0", "gru"), MIX),
                (("gather", 0, 0), (1, "att0", "gru", slice(0, 1)), GRU),
                (("gates", 0, 0), (1, "att0", "gru", slice(1, None)), GRU)]
        for l in range(GRU_LAYERS):
            if l:
                plan += [(("gather", 0, l), None, GRU), (("back", 1, l - 1), None, GRU), (("gates", 0, l), None, GRU)]
            plan += [(("gather", 1, l), None, GRU), (("back", 0, l), None, GRU),
                     (("gates", 1, l), (0, "gru", "att2") if l == GRU_LAYERS - 1 else None, GRU)]
        plan += [(("back", 1, GRU_LAYERS - 1), None, GRU),
                 (("mix", 0, "att2"), (1, "gru", "att2"), MIX),
                 (("mix", 1, "att2"), (0, "att2", "att3"), MIX),
                 (("mix", 0, "att3"), (1, "att2", "att3"), MIX),
                 (("mix", 1, "att3"), (0, "att3", None), MIX),
                 (None, (1, "att3", None), MIX)]
        MAIN_STEPS = {"mix": NU + LAG, "gather": H, "gates": 2 * H, "back": H}

        def run(mains, chain):
            for main, beside, banks in plan:
                todo = list(chain_steps(*beside[1:])) if beside else []
                total, given = len(todo), 0
                if main:
                    stage = mains[main[0]](*main[1:])
                    n = MAIN_STEPS[main[0]]
                    for m in range(n):
                        next(stage)
                        while given * n < total * (m + 1):
                            chain(beside[0], beside[1], beside[2], banks, todo[given])
                            given += 1
                    next(stage, None)
                else:
                    for step in todo:
                        chain(beside[0], beside[1], beside[2], banks, step)

        plan_of_gates = [(m[1], m[2], h) for m, _, _ in plan if m and m[0] == "gates" for h in range(H)]
        norms = [(beside[0], beside[2]) for _, beside, _ in plan if beside and "stats" in chain_steps(*beside[1:])]
        previous = dict(zip(norms[1:], norms))

        def bank(b):
            return psum[:, b, :]

        def tile_of(ap, t):
            return ap[:, t * P:(t + 1) * P]

        def half_of(ap, h):
            return ap[:, h * HALF:(h + 1) * HALF]

        def acc(t):
            return psum[:, t // 3, (t % 3) * VW:(t % 3 + 1) * VW]

        def flat(ap):
            return ap.rearrange("p t d -> p (t d)")

        h_flat = flat(h_nat[:])
        unkept = [h_flat.bitcast(BF16)[:, n * N:(n + 1) * N] for n in range(2)]
        ATT = {"att0": 0, "att2": 1, "att3": 2}

        block = ctx.enter_context(nc.Block())

        @block.tensor
        def _(pe):
            pe.wait_ge(*ident_ready.at("ident"))
            pe.wait_ge(loaded_w, 16 * N_LOADS)

            def tr(b, src):
                return pe.transpose(bank(b)[:, 0:P], src, ident[:])

            tr(0, raw["W0"][:]).then_inc(*setup_pe.done("W0T"))
            tr(1, raw["W3"][:]).then_inc(*setup_pe.done("W3"))
            tr(2, raw["W2"][:]).then_inc(*setup_pe.done("W2T"))
            for g in range(3):
                tr(3 + g, raw["w_hh"][:, g, :]).then_inc(*setup_pe.done("w_hh", g))
            pe.wait_ge(*weights.at("copies1"))
            for g in range(3):
                tr(3 + g, raw["w_ih"][:, g, :]).then_inc(*setup_pe.done("w_ih", g))
            for l in range(GRU_LAYERS):
                tr(l, raw["weight"][:, l, :]).then_inc(*setup_pe.done("weight", l))
            pe.wait_ge(*weights.at("copies2"))
            for l in range(GRU_LAYERS):
                pe.matmul(bank(l)[:, 0:3 * D], raw["weightT"][:, l, :], raw["w_ihT"][:], start=True, stop=True).then_inc(*setup_pe.done("wg_in", l))
            pe.matmul(bank(3)[:, 0:P], raw["a_12"][:], raw["W0T"][:], start=True, stop=True).then_inc(*setup_pe.done("a12W"))
            pe.matmul(bank(4)[:, 1:2], raw["W0T"][:], raw["a_2"][:], start=True, stop=True)
            pe.matmul(bank(4)[:, 2:3], raw["W0T"][:], raw["a_1"][:], start=True, stop=True)
            pe.matmul(bank(4)[:, 3:4], raw["W2T"][:], raw["a2"][:, 0:1], start=True, stop=True)
            pe.matmul(bank(4)[:, 4:5], raw["W2T"][:], raw["a2"][:, 1:2], start=True, stop=True)
            pe.matmul(bank(4)[:, 5:6], raw["W3"][:], raw["ai_w"][:], start=True, stop=True)
            pe.matmul(bank(4)[:, 6:7], raw["W3"][:], raw["aj_w"][:], start=True, stop=True)
            pe.matmul(bank(4)[:, 7:8], raw["b_rep"][:], raw["aij"][:], start=True, stop=True).then_inc(*setup_pe.done("vectors"))
            pe.wait_ge(*weights.at("copies3"))
            pe.matmul(bank(5)[:, 0:P], raw["a12WT"][:], raw["W0T"][:], start=True, stop=True).then_inc(*setup_pe.done("g0"))
            pe.wait_ge(*weights.at("all"))

            busy = {}

            def take(*banks):
                for b in banks:
                    if b in busy:
                        pe.wait_ge(*busy.pop(b))

            def three(to, a, b, start=True, stop=True, group=True):
                (a_hi, a_lo), (b_hi, b_lo) = a, b
                pe.matmul(to, a_hi, b_hi, start=start, stop=False, skip_group_check=not group)
                pe.matmul(to, a_hi, b_lo, start=False, stop=False, skip_group_check=not group)
                return pe.matmul(to, a_lo, b_hi, start=False, stop=stop, skip_group_check=not group)

            def chain(k, prev, L, pairs, step):
                b0, b1 = pairs[0]
                what, h = step if isinstance(step, tuple) else (step, None)
                hT = (hT_hi[k], hT_lo[k])
                b = (b0, b1)[h] if h in range(H) else None
                if what == "turn":
                    take(b)
                    for t in range(h * TH, (h + 1) * TH):
                        pe.wait_ge(*act_s.at("h_nat", k, L, t))
                        m = pe.transpose(tile_of(bank(b), t - h * TH), h_nat[:, t, :], ident[:])
                    m.then_inc(*pe_s.done("turn", k, L, h))
                    busy[b] = act_s.at("hT", k, L, h)
                if what == "s":
                    take(b)
                    pe.wait_ge(*act_s.at("hT", k, L, h))
                    pe.matmul(psum[S_ROWS, b, :], v_s[:, ATT[L], :], half_of(extra[k], h), start=True, stop=True).then_inc(*pe_s.done("s", k, L, h))
                    busy[b] = dve_s.at("s2_row", k, L, h)
                if what in ("vals", "extra"):
                    take(b)
                    w = {"att0": w0_2 if what == "vals" else w0_1, "att2": w2, "att3": w3}[L]
                    for t in range(h * TH, (h + 1) * TH):
                        m = pe.matmul(tile_of(bank(b), t - h * TH), tile_of(extra[k], t), w[:], start=True, stop=True)
                    m.then_inc(*pe_s.done(what, k, L, h))
                    busy[b] = dve_s.at("vals", k, L, h) if L == "att3" else act_s.at(what, k, L, h)
                if what == "q":
                    take(b)
                    pe.wait_ge(*dve_s.at("hT_lo", k, L, h))
                    three(bank(b), (g0[0][:], g0[1][:]), (half_of(hT[0], h), half_of(hT[1], h))).then_inc(*pe_s.done("q", k, h))
                    busy[b] = dve_s.at("q_lo", k, h)
                if what == "s_col":
                    take(b0)
                    for h in range(H):
                        pe.wait_ge(*dve_s.at("s1_row", k, L, h))
                    for t in range(T):
                        m = pe.matmul(psum[:, b0, 2 * t:2 * t + 2], tile_of(rows_i[k][S1, :], t), rows_j[k][S1, 0:2], start=True, stop=True)
                    m.then_inc(*pe_s.done("s_col", k, L))
                    busy[b0] = dve_s.at("s_col", k, L)
                if what == "s2":
                    for h in range(H):
                        b = (b0, b1)[h]
                        take(b)
                        pe.wait_ge(*dve_s.at("s2_row", k, L, h))
                        m = pe.matmul(bank(b), rows_i[k][S2, 0:P], half_of(rows_j[k][S2, :], h), start=True, stop=True)
                        busy[b] = dve_s.at("top", k, L, T - 1)
                    m.then_inc(*pe_s.done("s2", k, L))
                if what == "top" and L == "att0":
                    t = h
                    b = pairs[t % len(pairs)]
                    for h in range(H):
                        if t == 0:
                            pe.wait_ge(*dve_s.at("q_lo", k, h))
                        take(b[h])
                        three(bank(b[h]), (tile_of(part_hi[k], t), tile_of(part_lo[k], t)), (half_of(hT[0], h), half_of(hT[1], h)), stop=False)
                        m = pe.matmul(bank(b[h]), rows_i[k][S2, 0:P], half_of(rows_j[k][S2, :], h), start=False, stop=True)
                        busy[b[h]] = dve_s.at("top", k, L, t)
                    m.then_inc(*pe_s.done("qh", k, t))
                if what == "c_row":
                    pe.wait_ge(*dve_s.at("c_cols", k, L))
                    for h in range(H):
                        b = (b0, b1)[h]
                        take(b)
                        for t in range(h * TH, (h + 1) * TH):
                            m = pe.matmul(psum[0:2, b, (t - h * TH) * P:(t - h * TH + 1) * P], c_cols[k][:, t, :].bitcast(F32), ident[:], start=True, stop=True)
                        m.then_inc(*pe_s.done("c_row", k, L, h))
                        busy[b] = act_s.at("c_row", k, L, h)

            def mix(k, L):
                for h in range(H):
                    pe.wait_ge(*act_s.at("c_row", k, L, h))
                    pe.wait_ge(*(dve_s if L == "att3" else act_s).at("vals", k, L, h))
                rows = ALL_ROWS if L == "att2" else S_ROWS

                def logits(u):
                    t, h = UNITS[u]
                    b = Y_BANKS[u % 3]
                    take(b)
                    for i in range(TH):
                        pe.matmul(tile_of(bank(b), i), tile_of(mask[k][:, h * TH + i, :], t), ident_b[:],
                                  start=i == 0, stop=False, skip_group_check=True)
                    if L == "att0":
                        three(bank(b), (tile_of(hT_hi[k], t), tile_of(hT_lo[k], t)), (half_of(part_hi[k], h), half_of(part_lo[k], h)),
                              start=False, stop=False, group=False)
                    pe.matmul(bank(b), tile_of(rows_j[k][rows, :], t), half_of(rows_i[k][rows, :], h), start=False, stop=True,
                              skip_group_check=True).then_inc(*pe_s.done("logits", k, L, u))
                    busy[b] = act_s.at("probs", k, L, u) if L == "att2" else dve_s.at("leaky", k, L, u)

                def less_top(u):
                    t, h = UNITS[u]
                    pe.wait_ge(*act_s.at("relu", k, L, u))
                    pe.matmul(bank(Y_BANKS[u % 3]), tile_of(rows_j[k][C, :], t), half_of(rows_i[k][C, :], h), start=False, stop=True,
                              skip_group_check=True).then_inc(*pe_s.done("less_top", k, L, u))

                def weigh(u):
                    t, h = UNITS[u]
                    pe.wait_ge(*act_s.at("probs", k, L, u))
                    if u == 0:
                        take(0, 1, 2)
                    for i in range(TH):
                        o = h * TH + i
                        m = pe.matmul(acc(o), tile_of(ring[:, u % RING, :], i), vals[k][:, t, :], start=t == 0 and o % 3 == 0, stop=t == T - 1, skip_group_check=True)
                    m.then_inc(*pe_s.done("weighed", k, L, u))

                for s in range(NU + LAG):
                    if s < NU:
                        logits(s)
                    if L != "att2" and 1 <= s <= NU:
                        less_top(s - 1)
                    if s >= LAG:
                        weigh(s - LAG)
                    if s == NU + LAG - 1:
                        for b in range(3):
                            busy[b] = dve_s.at("mixed", k, L)
                    yield

            def gather(k, l):
                for h in range(H):
                    take(h)
                    for t in range(T):
                        if h == 0 and l == 0:
                            pe.wait_ge(*dve_s.at("edges", k, t))
                            if t == 0:
                                pe.wait_ge(*dve_s.at("part_lo", k, "gru"))
                        elif h == 0 and t % TH == 0:
                            pe.wait_ge(*act_s.at("nat_hi", k, l - 1, t // TH))
                            pe.wait_ge(*dve_s.at("nat_lo", k, l - 1, t // TH))
                        for part in (part_hi, part_lo):
                            m = pe.matmul(bank(h), tile_of(part[k], t), edges[k][:, t, h * HALF:(h + 1) * HALF],
                                          start=t == 0 and part is part_hi, stop=t == T - 1 and part is part_lo)
                    m.then_inc(*pe_s.done("sum", k, l, h))
                    busy[h] = dve_s.at("sum_lo", k, l, h)
                    yield

            def gates(k, l):
                for h in range(H):
                    if l == 0:
                        pe.wait_ge(*dve_s.at("hT_lo", k, "gru", h))
                    else:
                        pe.wait_ge(*act_s.at("state_hi", k, l - 1, h))
                        pe.wait_ge(*dve_s.at("state_lo", k, l - 1, h))
                    inp = (half_of(sum_hi[k], h), half_of(sum_lo[k], h))
                    hid = (half_of(hT_hi[k], h), half_of(hT_lo[k], h))

                    def w_in(g):
                        return tuple(w[:, l, g * D:(g + 1) * D] for w in wg_in)

                    def w_h(g):
                        return tuple(w[:, g * D:(g + 1) * D] for w in wg_h)

                    take(6)
                    three(bank(6), w_h(2), hid).then_inc(*pe_s.done("gate", k, l, h, 2))
                    busy[6] = act_s.at("gate", k, l, h, 2)
                    for g in range(2):
                        take(4 + g)
                        three(bank(4 + g), w_h(g), hid, stop=False)
                        if g == 0:
                            pe.wait_ge(*dve_s.at("sum_lo", k, l, h))
                        three(bank(4 + g), w_in(g), inp, start=False).then_inc(*pe_s.done("gate", k, l, h, g))
                        busy[4 + g] = act_s.at("gate", k, l, h, g)
                    yield
                    take(7)
                    three(bank(7), w_in(2), inp).then_inc(*pe_s.done("gate", k, l, h, 3))
                    busy[7] = dve_s.at("n_sum", k, l, h)
                    yield

            def back(k, l):
                for h in range(H):
                    pe.wait_ge(*dve_s.at("state", k, l, h))
                    take(h)
                    for i in range(TH):
                        m = pe.transpose(tile_of(bank(h), i), tile_of(extra[k], h * TH + i), ident[:])
                    m.then_inc(*pe_s.done("nat", k, l, h))
                    busy[h] = dve_s.at("nat_lo", k, l, h) if l < GRU_LAYERS - 1 else dve_s.at("x_gru", k, h)
                    yield

            with pe.Fori(0, PAIRS) as pair:
                run({"mix": mix, "gather": gather, "gates": gates, "back": back}, chain)
                pe.drain().then_inc(arrived, 1)
                pe.wait_ge(go, pair + 1)

        @block.scalar
        def _(act):
            def chain(k, prev, L, pairs, step):
                b0, b1 = pairs[0]
                what, h = step if isinstance(step, tuple) else (step, None)
                if what == "below":
                    act.wait_ge(*dve_s.at("mixed", k, prev))
                    act.activation(h_flat, extra[k][:], ACT.Relu, scale=-1.0).then_inc(*act_s.done("below", k, prev))
                if what == "elu_exp":
                    act.wait_ge(*act_s.at("below", k, prev))
                    act.activation(h_flat, h_flat, ACT.Exp, scale=-1.0).then_inc(*act_s.done("elu_exp", k, prev))
                if what == "h_nat":
                    if h == 0:
                        act.wait_ge(*dve_s.at("shift", k, L))
                    for t in (h, h + 1):
                        act.activation(h_nat[:, t, :], xs[k][:, t, :], ACT.Relu, bias=shift[:, t:t + 1], scale=rstd[:, t:t + 1]).then_inc(*act_s.done("h_nat", k, L, t))
                if what == "turned":
                    act.wait_ge(*pe_s.at("turn", k, L, h))
                    act.activation(half_of(extra[k], h), bank((b0, b1)[h]), ACT.Copy).then_inc(*act_s.done("hT", k, L, h))
                if what == "s_out":
                    if L == "att3":
                        act.wait_ge(*dve_s.at("s_biased", k, h))
                    act.wait_ge(*pe_s.at("s", k, L, h))
                    act.activation(half_of(s_hi[S_ROWS, :], h), psum[S_ROWS, (b0, b1)[h], :], ACT.Copy).then_inc(*act_s.done("s_hi", k, L, h))
                if what == "vals_out" and L != "att3":
                    act.wait_ge(*pe_s.at("vals", k, L, h))
                    act.activation(vals[k][:, h * TH:(h + 1) * TH, 0:D], bank((b0, b1)[h]).rearrange("p (t d) -> p t d", d=D), ACT.Copy).then_inc(*act_s.done("vals", k, L, h))
                if what == "q_out":
                    act.wait_ge(*pe_s.at("q", k, h))
                    act.activation(half_of(part_hi[k], h), bank((b0, b1)[h]), ACT.Copy).then_inc(*act_s.done("q_hi", k, h))
                if what == "extra_out":
                    act.wait_ge(*pe_s.at("extra", k, L, h))
                    act.activation(half_of(extra[k], h), bank((b0, b1)[h]), ACT.Copy).then_inc(*act_s.done("extra", k, L, h))
                if what == "c_row_out":
                    for h in range(H):
                        act.wait_ge(*pe_s.at("c_row", k, L, h))
                        act.activation(half_of(rows_i[k][C, :], h), psum[0:2, (b0, b1)[h], :], ACT.Copy).then_inc(*act_s.done("c_row", k, L, h))

            def mix(k, L):
                if L == "att2" and k == 0:
                    act.wait_ge(*dve_s.at("state", 1, GRU_LAYERS - 1, H - 1))

                def ring_free(u):
                    if u >= RING:
                        act.wait_ge(*pe_s.at("weighed", k, L, u - RING))

                for s in range(NU + LAG):
                    y, p = ring[:, s % RING, :], ring[:, (s - 1) % RING, :]
                    if L == "att2" and s < NU:
                        act.wait_ge(*pe_s.at("logits", k, L, s))
                        ring_free(s)
                        act.activation(y, bank(Y_BANKS[s % 3]), ACT.Exp).then_inc(*act_s.done("probs", k, L, s))
                    if L != "att2" and s < NU:
                        act.wait_ge(*pe_s.at("logits", k, L, s))
                        ring_free(s)
                        act.activation(y, bank(Y_BANKS[s % 3]), ACT.Relu, scale=STEEP).then_inc(*act_s.done("relu", k, L, s))
                    if L != "att2" and 1 <= s <= NU:
                        act.wait_ge(*dve_s.at("leaky", k, L, s - 1))
                        act.activation(p, p, ACT.Exp, scale=ALPHA).then_inc(*act_s.done("probs", k, L, s - 1))
                    yield

            def gather(k, l):
                for h in range(H):
                    yield
                for h in range(H):
                    act.wait_ge(*pe_s.at("sum", k, l, h))
                    act.activation(half_of(sum_hi[k], h), bank(h), ACT.Copy).then_inc(*act_s.done("sum_hi", k, l, h))

            def gates(k, l):
                for h in range(H):
                    at = plan_of_gates.index((k, l, h))
                    if at:
                        act.wait_ge(*dve_s.at("state", *plan_of_gates[at - 1]))
                    act.wait_ge(*pe_s.at("gate", k, l, h, 2))
                    act.activation(gru_hn, bank(6), ACT.Identity, bias=gate_bias[:, 2:3], scale=0.5).then_inc(*act_s.done("gate", k, l, h, 2))
                    act.wait_ge(*pe_s.at("gate", k, l, h, 0))
                    act.activation(gru_r, bank(4), ACT.Tanh, bias=gate_bias[:, 0:1], scale=0.5).then_inc(*act_s.done("gate", k, l, h, 0))
                    act.wait_ge(*pe_s.at("gate", k, l, h, 1))
                    act.activation(gru_z, bank(5), ACT.Tanh, bias=gate_bias[:, 1:2], scale=0.5).then_inc(*act_s.done("gate", k, l, h, 1))
                    yield
                    act.wait_ge(*dve_s.at("n_sum", k, l, h))
                    act.activation(gru_n, gru_hn, ACT.Tanh, bias=gate_bias[:, 3:4]).then_inc(*act_s.done("n", k, l, h))
                    act.wait_ge(*dve_s.at("state", k, l, h))
                    act.activation(half_of(hT_hi[k], h), half_of(extra[k], h), ACT.Copy).then_inc(*act_s.done("state_hi", k, l, h))
                    yield

            def back(k, l):
                for h in range(H):
                    if l < GRU_LAYERS - 1:
                        act.wait_ge(*pe_s.at("nat", k, l, h))
                        act.activation(half_of(part_hi[k], h), bank(h), ACT.Copy).then_inc(*act_s.done("nat_hi", k, l, h))
                    yield

            with act.Fori(0, PAIRS) as pair:
                run({"mix": mix, "gather": gather, "gates": gates, "back": back}, chain)
                act.drain().then_inc(arrived, 1)
                act.wait_ge(go, pair + 1)

        @block.vector
        def _(dve):
            def split(dst, src, *name):
                dve.tensor_copy(dst[0], src).then_inc(*weights.done(*name, "hi"))
                dve.wait_ge(*weights.last())
                dve.tensor_tensor(dst[1], src, dst[0].bitcast(F32), ALU.subtract).then_inc(*weights.done(*name))

            def copy_w(dst, src, step, label=None):
                dve.wait_ge(*setup_pe.at(*step))
                dve.tensor_copy(dst, src).then_inc(*weights.done(*(label or ("copied",) + step)))

            dve.wait_ge(loaded_w, 16 * N_LOADS)
            dve.wait_ge(*ident_ready.at("ident"))
            dve.tensor_copy(ident_b[:], ident[:]).then_inc(*weights.done("ident_b"))
            dve.tensor_copy(raw["b_rep"][:], raw["W_b"][:].broadcast_to([P, P])).then_inc(*weights.done("b_rep"))
            dve.tensor_tensor(raw["aij"][:], raw["ai_w"][:], raw["aj_w"][:], ALU.add).then_inc(*weights.done("aij"))
            for g in range(2):
                dve.tensor_scalar(gate_bias[:, g:g + 1], b_ih[:, g:g + 1], b_hh[:, g:g + 1], 0.5, ALU.add, ALU.mult).then_inc(*weights.done("gate_bias", g))
            dve.tensor_scalar(gate_bias[:, 2:3], b_hh[:, 2:3], 0.5, None, ALU.mult).then_inc(*weights.done("gate_bias", 2))
            dve.tensor_copy(gate_bias[:, 3:4], b_ih[:, 2:3]).then_inc(*weights.done("gate_bias", 3))
            copy_w(raw["W0T"][:], bank(0)[:, 0:P], ("W0T",))
            copy_w(w3[:], bank(1)[:, 0:P], ("W3",))
            dve.tensor_copy(w2[:], raw["W2"][:]).then_inc(*weights.done("w2"))
            copy_w(raw["W2T"][:], bank(2)[:, 0:P], ("W2T",))
            for g in range(3):
                dve.wait_ge(*setup_pe.at("w_hh", g))
                split(tuple(w[:, g * D:(g + 1) * D] for w in wg_h), bank(3 + g)[:, 0:P], "copies1")
            for g in range(3):
                copy_w(raw["w_ihT"][:, g * D:(g + 1) * D], bank(3 + g)[:, 0:P], ("w_ih", g))
            for l in range(GRU_LAYERS):
                copy_w(raw["weightT"][:, l, :], bank(l)[:, 0:P], ("weight", l), ("copies2",))
            for l in range(GRU_LAYERS):
                dve.wait_ge(*setup_pe.at("wg_in", l))
                split(tuple(w[:, l, :] for w in wg_in), bank(l)[:, 0:3 * D], "wg_in", l)
            copy_w(raw["a12WT"][:], bank(3)[:, 0:P], ("a12W",), ("copies3",))
            dve.memset(v_s[:], 0.0).then_inc(*weights.done("v_s", "zero"))
            dve.memset(lo_row[:], 0.0).then_inc(*weights.done("lo_row", "zero"))
            dve.memset(const3[:], 0.0).then_inc(*weights.done("const3", "zero"))
            for k in SLOTS:
                for rows in (rows_i[k], rows_j[k]):
                    dve.memset(rows[:].bitcast(F32), 0.0).then_inc(*weights.done("rows", "zero"))
            dve.wait_ge(*weights.last())
            for k in SLOTS:
                for to, pair in ((rows_j, S1), (rows_i, S2), (rows_j, C)):
                    dve.memset(to[k][pair, :].bitcast(F32), 1.0).then_inc(*weights.done("rows", "one"))
            for pair in (S1, S2):
                dve.memset(lo_row[pair, :], 1.0).then_inc(*weights.done("lo_row", "one"))
            dve.wait_ge(*weights.last())
            for k in SLOTS:
                for to, pair in ((rows_j, S1), (rows_i, S2)):
                    dve.memset(to[k][pair.start:pair.start + 1, :].bitcast(F32), -1.0).then_inc(*weights.done("rows", "minus"))
            for pair in (S1, S2):
                dve.memset(lo_row[pair.start:pair.start + 1, :], 0.0).then_inc(*weights.done("lo_row"))
            dve.wait_ge(*setup_pe.at("vectors"))
            for at, c in ((0, 0), (1, 0), (32, 1), (33, 1)):
                dve.tensor_copy(v_s[:, :, at], psum[:, 4, 1:7].rearrange("p (l c) -> p l c", c=2)[:, :, c]).then_inc(*weights.done("v_s"))
            dve.tensor_scalar(const3[S1, :], psum[S1, 4, 7:8], raw["aib"][S1, 0:1], raw["ajb"][S1, 0:1], ALU.add, ALU.add).then_inc(*weights.done("const3"))
            dve.wait_ge(*setup_pe.at("g0"))
            split((g0[0][:], g0[1][:]), bank(5)[:, 0:P], "g0")
            dve.engine_nop().then_inc(*weights.done("all"))
            dve.wait_ge(*weights.last())

            def chain(k, prev, L, pairs, step):
                b0, b1 = pairs[0]
                what, h = step if isinstance(step, tuple) else (step, None)
                xk = flat(xs[k][:])
                if what == "mixed":
                    dve.wait_ge(*pe_s.at("weighed", k, prev, NU - 1))
                    for b in range(3):
                        n = min(3, T - 3 * b)
                        s = psum[:, b, 0:n * VW].rearrange("p (t w) -> p t w", w=VW)[:, :, D]
                        m = dve.reciprocal(rsum[k][:, 3 * b:3 * b + n], s)
                    m.then_inc(*dve_s.done("rsum", k, prev))
                    dve.wait_ge(*dve_s.last())
                    for t in range(T):
                        dst = tile_of(extra[k], t)
                        if prev == "att0":
                            m = dve.scalar_tensor_tensor(dst, acc(t)[:, 0:D], rsum[k][:, t:t + 1], dst, ALU.mult, ALU.add)
                        else:
                            m = dve.tensor_scalar(dst, acc(t)[:, 0:D], rsum[k][:, t:t + 1], None, ALU.mult)
                    m.then_inc(*dve_s.done("mixed", k, prev))
                if what == "x":
                    dve.wait_ge(*act_s.at("elu_exp", k, prev))
                    dve.scalar_tensor_tensor(xk, h_flat, -1.0, xk, ALU.add, ALU.add).then_inc(*dve_s.done("x_part", k, prev))
                    dve.wait_ge(*dve_s.last())
                    dve.scalar_tensor_tensor(xk, extra[k][:], 0.0, xk, ALU.max, ALU.add).then_inc(*dve_s.done("x", k, prev))
                if what == "stats":
                    if L == "att0":
                        dve.wait_ge(x_in[k], 16 * (loop[0] + 1))
                    else:
                        dve.wait_ge(*(dve_s.at("x_gru", k, H - 1) if prev == "gru" else dve_s.at("x", k, prev)))
                    for t in range(T):
                        m = dve.bn_stats(stats[:, t, :], xs[k][:, t, :])
                    m.then_inc(*dve_s.done("stats", k, L))
                if what == "rstd":
                    dve.wait_ge(*dve_s.at("stats", k, L))
                    for t in range(T):
                        m = dve.bn_aggr(mean_var[:, t, :], stats[:, t, :])
                    m.then_inc(*dve_s.done("mean_var", k, L))
                if what == "shift":
                    if L == "att0" and k == 0:
                        masks(k, range(T))
                    dve.wait_ge(*pool_s.at("rstd", k, L))
                    if (k, L) in previous:
                        pk, pL = previous[(k, L)]
                        dve.wait_ge(*act_s.at("h_nat", pk, pL, T - 1))
                    dve.scalar_tensor_tensor(shift[:], mean_var[:, :, 0], -1.0, rstd[:], ALU.mult, ALU.mult).then_inc(*dve_s.done("shift", k, L))
                if what == "part_hi":
                    dve.wait_ge(*act_s.at("h_nat", k, L, T - 1))
                    dve.tensor_copy(part_hi[k][:], h_flat).then_inc(*dve_s.done("part_hi", k, L))
                if what == "part_lo":
                    dve.wait_ge(*dve_s.at("part_hi", k, L))
                    dve.tensor_tensor(part_lo[k][:], h_flat, part_hi[k][:].bitcast(F32), ALU.subtract).then_inc(*dve_s.done("part_lo", k, L))
                if what == "turned" and L == "att0" and k == 1:
                    masks(k, range(h * TH, (h + 1) * TH))
                if what == "split":
                    dve.wait_ge(*act_s.at("hT", k, L, h))
                    dve.tensor_copy(half_of(hT_hi[k], h), half_of(extra[k], h)).then_inc(*dve_s.done("hT_hi", k, L, h))
                    dve.wait_ge(*dve_s.last())
                    dve.tensor_tensor(half_of(hT_lo[k], h), half_of(extra[k], h), half_of(hT_hi[k], h).bitcast(F32), ALU.subtract).then_inc(*dve_s.done("hT_lo", k, L, h))
                if what == "s_out":
                    b = (b0, b1)[h]
                    if L == "att3":
                        dve.wait_ge(*pe_s.at("s", k, L, h))
                        dve.tensor_scalar(psum[S_ROWS, b, :], psum[S_ROWS, b, :], const3[S_ROWS, 0:1], None, ALU.add).then_inc(*dve_s.done("s_biased", k, h))
                    dve.wait_ge(*act_s.at("s_hi", k, L, h))
                    for to, pair, name in ((rows_i, S1, "s1_row"), (rows_j, S2, "s2_row")):
                        dve.scalar_tensor_tensor(half_of(to[k][pair, :], h), psum[pair, b, :], lo_row[pair, 0:1], half_of(s_hi[pair, :], h).bitcast(F32),
                                                 ALU.mult, ALU.subtract).then_inc(*dve_s.done(name, k, L, h))
                if what == "s_col_out":
                    dve.wait_ge(*pe_s.at("s_col", k, L))
                    dve.tensor_copy(s_col[k][:], psum[:, b0, 0:2 * T].rearrange("p (t c) -> p t c", c=2)[:, :, 0]).then_inc(*dve_s.done("s_col", k, L))
                if what == "vals_out":
                    if h == 0:
                        dve.memset(vals[k][:, :, D:VW], 1.0).then_inc(*dve_s.done("ones", k, L))
                    if L == "att3":
                        r = slice(h * TH, (h + 1) * TH)
                        dve.wait_ge(*pe_s.at("vals", k, L, h))
                        dve.tensor_tensor(vals[k][:, r, 0:D], bank((b0, b1)[h]).rearrange("p (t d) -> p t d", d=D),
                                          bias3[:].rearrange("p (o d) -> p o d", o=1).broadcast_to([P, TH, D]), ALU.add).then_inc(*dve_s.done("vals", k, L, h))
                if what == "q_out":
                    dve.wait_ge(*act_s.at("q_hi", k, h))
                    dve.tensor_tensor(half_of(part_lo[k], h), bank((b0, b1)[h]), half_of(part_hi[k], h).bitcast(F32), ALU.subtract).then_inc(*dve_s.done("q_lo", k, h))
                if what == "top":
                    t = h
                    b = pairs[t % len(pairs)][0] if L == "att0" else b0
                    dve.wait_ge(*(pe_s.at("qh", k, t) if L == "att0" else pe_s.at("s2", k, L)))
                    if t >= 2:
                        dve.wait_ge(*dve_s.at("top", k, L, t - 2))
                    dve.tensor_tensor_reduce(unkept[t % 2], psum[:, b:b + 2, :].rearrange("p b n -> p (b n)"), mask[k][:, t, :], 1.0, LOWEST,
                                             ALU.add, ALU.max, top[k][:, t:t + 1]).then_inc(*dve_s.done("top", k, L, t))
                if what == "c_col":
                    dve.wait_ge(*dve_s.at("top", k, L, T - 1))
                    dve.tensor_tensor(top[k][:], top[k][:], s_col[k][:], ALU.add).then_inc(*dve_s.done("row_top", k, L))
                    dve.wait_ge(*dve_s.last())
                    if L == "att2":
                        dve.tensor_scalar(c_col[k][:], top[k][:], -1.0, None, ALU.mult).then_inc(*dve_s.done("c_col", k, L))
                    else:
                        dve.tensor_scalar(top2[k][:], top[k][:], 0.0, -STEEP, ALU.max, ALU.mult).then_inc(*dve_s.done("top2", k, L))
                        dve.wait_ge(*dve_s.last())
                        dve.tensor_tensor(c_col[k][:], top2[k][:], top[k][:], ALU.subtract).then_inc(*dve_s.done("c_col", k, L))
                if what == "c_cols":
                    dve.wait_ge(*dve_s.at("c_col", k, L))
                    to = c_cols[k]
                    dve.tensor_copy(to[:, :, 0], c_col[k][:]).then_inc(*dve_s.done("c_hi", k, L))
                    dve.wait_ge(*dve_s.last())
                    dve.tensor_tensor(to[:, :, 1], c_col[k][:], to[:, :, 0].bitcast(F32), ALU.subtract).then_inc(*dve_s.done("c_cols", k, L))

            def masks(k, tiles):
                for t in tiles:
                    if t % CHUNK == 0:
                        dve.wait_ge(adj_loaded[k][t // CHUNK], 16 * (loop[0] + 1))
                    dve.tensor_scalar(mask[k][:, t, :], adj_in[k][:, t, :], 0, MASKED, ALU.is_le, ALU.mult).then_inc(*dve_s.done("mask", k, t))

            def mix(k, L):
                for s in range(NU + LAG):
                    if L == "att0" and s % H == 0 and s < NU:
                        t = s // H
                        dve.tensor_scalar(edges[k][:, t, :], adj_in[k][:, t, :], 0, None, ALU.not_equal).then_inc(*dve_s.done("edges", k, t))
                    if L != "att2" and 1 <= s <= NU:
                        u = s - 1
                        dve.wait_ge(*pe_s.at("less_top", k, L, u))
                        dve.tensor_tensor(ring[:, u % RING, :], bank(Y_BANKS[u % 3]), ring[:, u % RING, :], ALU.add).then_inc(*dve_s.done("leaky", k, L, u))
                    yield

            def gather(k, l):
                for h in range(H):
                    yield
                for h in range(H):
                    dve.wait_ge(*act_s.at("sum_hi", k, l, h))
                    dve.tensor_tensor(half_of(sum_lo[k], h), bank(h), half_of(sum_hi[k], h).bitcast(F32), ALU.subtract).then_inc(*dve_s.done("sum_lo", k, l, h))

            def gates(k, l):
                for h in range(H):
                    yield
                    dve.wait_ge(*act_s.at("gate", k, l, h, 0))
                    dve.scalar_tensor_tensor(gru_hn, gru_r, 1.0, gru_hn, ALU.add, ALU.mult).then_inc(*dve_s.done("r_n", k, l, h))
                    dve.wait_ge(*pe_s.at("gate", k, l, h, 3))
                    dve.wait_ge(*dve_s.last())
                    dve.tensor_tensor(gru_hn, bank(7), gru_hn, ALU.add).then_inc(*dve_s.done("n_sum", k, l, h))
                    dve.wait_ge(*act_s.at("n", k, l, h))
                    dve.tensor_tensor(gru_r, half_of(extra[k], h), gru_n, ALU.subtract).then_inc(*dve_s.done("h_less_n", k, l, h))
                    dve.wait_ge(*dve_s.last())
                    dve.scalar_tensor_tensor(gru_r, gru_z, 1.0, gru_r, ALU.add, ALU.mult).then_inc(*dve_s.done("z_part", k, l, h))
                    dve.wait_ge(*dve_s.last())
                    dve.scalar_tensor_tensor(half_of(extra[k], h), gru_r, 0.5, gru_n, ALU.mult, ALU.add).then_inc(*dve_s.done("state", k, l, h))
                    dve.wait_ge(*act_s.at("state_hi", k, l, h))
                    dve.tensor_tensor(half_of(hT_lo[k], h), half_of(extra[k], h), half_of(hT_hi[k], h).bitcast(F32), ALU.subtract).then_inc(*dve_s.done("state_lo", k, l, h))
                    yield

            def back(k, l):
                for h in range(H):
                    if l < GRU_LAYERS - 1:
                        dve.wait_ge(*act_s.at("nat_hi", k, l, h))
                        dve.tensor_tensor(half_of(part_lo[k], h), bank(h), half_of(part_hi[k], h).bitcast(F32), ALU.subtract).then_inc(*dve_s.done("nat_lo", k, l, h))
                    else:
                        dve.wait_ge(*pe_s.at("nat", k, l, h))
                        xk = half_of(flat(xs[k][:]), h)
                        dve.tensor_tensor(xk, bank(h), xk, ALU.add).then_inc(*dve_s.done("x_gru", k, h))
                    yield

            with dve.Fori(0, PAIRS) as pair:
                loop = [pair]
                run({"mix": mix, "gather": gather, "gates": gates, "back": back}, chain)
                dve.drain().then_inc(arrived, 1)
                dve.wait_ge(go, pair + 1)

        @block.gpsimd
        def _(pool):
            pool.memset(minus_half[:], -0.5).then_inc(*ident_ready.done("half"))
            pool.memset(ident[:], 0.0).then_inc(*ident_ready.done("zero"))
            pool.wait_ge(*ident_ready.last())
            pool.affine_select(out=ident[:], in_=ident[:], compare_op=ALU.not_equal, fill=1.0, base=0,
                               pattern=[[-1, P]], channel_multiplier=1).then_inc(*ident_ready.done("ident"))

            def chain(k, prev, L, pairs, step):
                if step == "shift":
                    pool.wait_ge(*dve_s.at("mean_var", k, L))
                    pool.tensor_scalar(rstd[:], mean_var[:, :, 1], EPS, 1.0, ALU.add, ALU.mult).then_inc(*pool_s.done("var", k, L))
                    pool.wait_ge(*pool_s.last())
                    pool.tensor_tensor(rstd[:], rstd[:], minus_half[:], ALU.pow).then_inc(*pool_s.done("rstd", k, L))

            def nothing(name):
                def stage(*_):
                    for _ in range(MAIN_STEPS[name]):
                        yield
                return stage

            with pool.Fori(0, PAIRS) as pair:
                run({name: nothing(name) for name in MAIN_STEPS}, chain)
                pool.drain().then_inc(arrived, 1)
                pool.wait_ge(go, pair + 1)

        @block.sync
        def _(sp):
            def load_x(k, pair):
                sp.dma_start(xs[k][:], x.rearrange("g (t p) d -> g p t d", p=P)[bass.ds(2 * pair + k, 1)].rearrange("o p t d -> (o p) t d")).then_inc(x_in[k], 16)

            def load_adj(k, pair):
                g = adj.rearrange("g (t p) n -> g p t n", p=P)[bass.ds(2 * pair + k, 1)].rearrange("o p t n -> (o p) t n")
                for c in range(CHUNKS):
                    sp.dma_start(adj_in[k][:, c * CHUNK:(c + 1) * CHUNK, :], g[:, c * CHUNK:(c + 1) * CHUNK, :]).then_inc(adj_loaded[k][c], 16)

            def store(k, pair):
                sp.wait_ge(*dve_s.at("x", k, "att3"))
                sp.dma_start(out.rearrange("g (t p) d -> g p t d", p=P)[bass.ds(2 * pair + k, 1)].rearrange("o p t d -> (o p) t d"), xs[k][:]).then_inc(stored, 16)
                sp.wait_ge(stored, 16 * (k + 1))

            for k in SLOTS:
                load_x(k, 0)
            for dst, src in loads:
                sp.dma_start(dst, src).then_inc(loaded_w, 16)
            load_adj(0, 0)
            sp.wait_ge(*weights.at("all"))
            load_adj(1, 0)

            def end_of_pass():
                sp.wait_ge(arrived, 4)
                sp.sem_clear(range(per_pass[0].num, per_pass[-1].num + 1))
                sp.sem_inc(go, 1)

            with sp.Fori(0, PAIRS - 1) as pair:
                for k in SLOTS:
                    sp.wait_ge(*pe_s.at("sum", k, GRU_LAYERS - 1, H - 1))
                    load_adj(k, pair + 1)
                for k in SLOTS:
                    store(k, pair)
                    load_x(k, pair + 1)
                end_of_pass()
            for k in SLOTS:
                store(k, PAIRS - 1)
            end_of_pass()


_ARGS = {
    "x": "x", "adj": "adj",
    "p0": {"W": "L0_gnn_W", "a_1": "L0_gnn_a_1", "a_2": "L0_gnn_a_2", "a_12": "L0_gnn_a_12", "W_1": "L0_gnn_W_1", "W_2": "L0_gnn_W_2"},
    "p1": {"weight": "L1_gnn_weight", "w_ih": "L1_gnn_w_ih", "w_hh": "L1_gnn_w_hh", "b_ih": "L1_gnn_b_ih", "b_hh": "L1_gnn_b_hh"},
    "p2": {"W": "L2_gnn_W", "a": "L2_gnn_a"},
    "p3": {"W_w": "L3_gnn_W_w", "W_b": "L3_gnn_W_b", "ai_w": "L3_gnn_ai_w", "ai_b": "L3_gnn_ai_b", "aj_w": "L3_gnn_aj_w", "aj_b": "L3_gnn_aj_b"},
}


def kernel(**inputs):
    import concourse.bacc as _bacc
    from concourse.bass_utils import run_bass_kernel_spmd as _run

    counts = {}
    for _ in range(2):
        nc = _bacc.Bacc("TRN2", target_bir_lowering=False, num_devices=1)
        arrays = {}

        def dram(name):
            a = np.ascontiguousarray(inputs[name])
            arrays[f"in_{name}"] = a
            return nc.dram_tensor(f"in_{name}", a.shape, mybir.dt.from_np(a.dtype), kind="ExternalInput").ap()

        args = {k: dram(v) if isinstance(v, str) else {n: dram(m) for n, m in v.items()} for k, v in _ARGS.items()}
        args["out"] = nc.dram_tensor("out_x", args["x"].shape, F32, kind="ExternalOutput").ap()
        build(nc, counts, **args)
    r = _run(nc, [arrays], core_ids=[0])
    return r.results[0]["out_x"]
```

```python
from contextlib import ExitStack

import numpy as np

import concourse.bass as bass
from concourse import mybir
from concourse.alu_op_type import AluOpType as ALU

ACT = mybir.ActivationFunctionType
F32 = mybir.dt.float32
F32R = mybir.dt.float32r
BF16 = mybir.dt.bfloat16
I32 = mybir.dt.int32

P = 128
HALF = 512
MASKED = -9.0e15
LOWEST = -3.0e38
EPS = 1e-5
ALPHA = 0.2
STEEP = (1.0 - ALPHA) / ALPHA


class Steps:

    def __init__(self, sem, counts):
        self.sem, self.counts, self.n, self.phase = sem, counts, 0, None

    def begin(self, phase):
        self.n, self.phase = 0, phase

    def done(self, *step):
        self.n += 1
        self.counts[self.phase, step] = self.n
        return self.sem, 1

    def at(self, *step):
        return self.sem, self.counts.get((self.phase, step), 1)

    def last(self):
        return self.sem, self.n


def build(nc, counts, x, adj, p0, p1, p2, p3, out):
    GRAPHS, N, D = x.shape
    T = N // P
    H = N // HALF
    TH = T // H
    PAIRS = GRAPHS // 2
    GRU_LAYERS = p1["weight"].shape[0]
    VW = D + 1
    CHUNK = 2
    CHUNKS = T // CHUNK
    SLOTS = range(2)
    assert D == P and GRAPHS % 2 == 0

    with ExitStack() as ctx:
        def sb(name, shape, dt=F32):
            return ctx.enter_context(nc.sbuf_tensor(name, shape, dt))

        def sem(name):
            return ctx.enter_context(nc.semaphore(name))

        def steps(name):
            return Steps(sem(name), counts.setdefault(name, {}))

        edge_bytes = T * N * 4
        base = (nc.sbuf_base + 31) // 32 * 32
        sb("edge_slab", [P, 2 * edge_bytes // 4 + 8], I32)
        adj_in = [nc.alloc_sbuf_tensor_at(f"adj_in{k}", [P, T, N], I32, offset=base + k * edge_bytes) for k in SLOTS]
        edges = [nc.alloc_sbuf_tensor_at(f"edges{k}", [P, T, N], F32R, offset=base + k * edge_bytes) for k in SLOTS]

        RING = 5
        ring = sb("ring", [P, RING, HALF])
        gru_r, gru_z, gru_hn, gru_n = (ring[:, i, :] for i in range(4))

        mask = [sb(f"mask{k}", [P, T, N], BF16) for k in SLOTS]
        xs = [sb(f"xs{k}", [P, T, D]) for k in SLOTS]
        extra = [sb(f"extra{k}", [P, N]) for k in SLOTS]
        hT_hi = [sb(f"hT_hi{k}", [P, N], F32R) for k in SLOTS]
        hT_lo = [sb(f"hT_lo{k}", [P, N], F32R) for k in SLOTS]
        part_hi = [sb(f"part_hi{k}", [P, N], F32R) for k in SLOTS]
        part_lo = [sb(f"part_lo{k}", [P, N], F32R) for k in SLOTS]
        sum_lo = [sb(f"sum_lo{k}", [P, N], F32R) for k in SLOTS]
        sum_hi, vals = [], []
        for k in SLOTS:
            at = (nc.sbuf_base + 31) // 32 * 32
            sb(f"vals_place{k}", [P, T * VW + 8])
            sum_hi.append(nc.alloc_sbuf_tensor_at(f"sum_hi{k}", [P, N], F32R, offset=at))
            vals.append(nc.alloc_sbuf_tensor_at(f"vals{k}", [P, T, VW], F32, offset=at))
        S1, S2, C = slice(0, 2), slice(32, 34), slice(64, 66)
        S_ROWS, ALL_ROWS = slice(0, 34), slice(0, 66)
        rows_i = [sb(f"rows_i{k}", [P, N], F32R) for k in SLOTS]
        rows_j = [sb(f"rows_j{k}", [P, N], F32R) for k in SLOTS]
        lo_row = sb("lo_row", [P, 1])
        at = (nc.sbuf_base + 31) // 32 * 32
        sb("h_place", [P, T * D + 8])
        h_nat = nc.alloc_sbuf_tensor_at("h_nat", [P, T, D], F32, offset=at)
        s_hi = nc.alloc_sbuf_tensor_at("s_hi", [P, N], F32R, offset=at)

        stats = sb("stats", [P, T, 6])
        mean_var = sb("mean_var", [P, T, 2])
        rstd = sb("rstd", [P, T])
        shift = sb("shift", [P, T])
        minus_half = sb("minus_half", [P, T])
        s_col = [sb(f"s_col{k}", [P, T]) for k in SLOTS]
        top = [sb(f"top{k}", [P, T, H]) for k in SLOTS]
        top2 = [sb(f"top2{k}", [P, T]) for k in SLOTS]
        c_col = [sb(f"c_col{k}", [P, T]) for k in SLOTS]
        rsum = [sb(f"rsum{k}", [P, T]) for k in SLOTS]
        c_cols = [sb(f"c_cols{k}", [P, T, 2], F32R) for k in SLOTS]

        ident_b = sb("ident_b", [P, P], BF16)
        ident = sb("ident", [P, P])

        def parts(name, shape):
            return sb(name + "_hi", shape, F32R), sb(name + "_lo", shape, F32R)

        w0_1, w0_2, w2, w3 = (sb(n, [P, D]) for n in ("w0_1", "w0_2", "w2", "w3"))
        bias3 = sb("bias3", [P, D])
        g0 = parts("g0", [P, D])
        v_s = sb("v_s", [P, 3, S2.stop])
        v0_s2 = v_s[:, 0, S2.start:S2.start + 1]
        const3 = sb("const3", [P, 1])
        wg_in = parts("wg_in", [P, GRU_LAYERS, 3 * D])
        wg_h = parts("wg_h", [P, 3 * D])
        b_ih = sb("b_ih", [P, 3])
        b_hh = sb("b_hh", [P, 3])
        gate_bias = sb("gate_bias", [P, 4])

        psum = ctx.enter_context(nc.psum_tensor("psum", [P, 8, HALF], F32))

        ident_ready = steps("ident_ready")
        weights = steps("weights_ready")
        setup_pe = steps("setup_products")
        loaded_w = sem("loaded_w")
        x_in = [sem(f"x_in{k}") for k in SLOTS]
        go = sem("next_pass")
        adj_loaded = [[sem(f"adj_loaded{k}_{c}") for c in range(CHUNKS)] for k in reversed(SLOTS)][::-1]
        arrived = sem("engines_arrived")
        pe_s = steps("pe_step")
        act_s = steps("act_step")
        dve_s = steps("dve_step")
        pool_s = steps("pool_step")
        stored = sem("stored")
        per_pass = adj_loaded[0] + [arrived, pe_s.sem, act_s.sem, dve_s.sem, pool_s.sem, stored]
        assert [s.num for s in per_pass] == list(range(per_pass[0].num, per_pass[0].num + len(per_pass)))

        setup_at = [base + edge_bytes]

        def raw_tile(name, shape):
            tile = nc.alloc_sbuf_tensor_at(name, shape, F32, offset=setup_at[0])
            setup_at[0] += (4 * int(np.prod(shape[1:])) + 31) // 32 * 32
            return tile

        raw = {n: raw_tile(f"raw_{n}", s) for n, s in {
            "W0": [P, D], "W0T": [P, D], "a_12": [P, D], "a12WT": [P, D], "W2": [P, D], "W2T": [P, D], "W3": [P, D],
            "w_ih": [P, 3, D], "w_ihT": [P, 3 * D], "w_hh": [P, 3, D], "weight": [P, GRU_LAYERS, D], "weightT": [P, GRU_LAYERS, D],
            "a_1": [P, 1], "a_2": [P, 1], "a2": [P, 2], "ai_w": [P, 1], "aj_w": [P, 1], "aij": [P, 1],
            "W_b": [P, 1], "b_rep": [P, D], "aib": [P, 1], "ajb": [P, 1]}.items()}

        def column(ap):
            return ap.rearrange("(p o) -> p o", o=1)

        def everywhere(ap, n):
            return ap.rearrange("(o n) -> o n", o=1).broadcast_to([P, n])

        loads = [
            (raw["W0"][:], p0["W"]), (raw["W2"][:], p2["W"]), (raw["W3"][:], p3["W_w"]), (raw["a_12"][:], p0["a_12"]),
            (raw["w_hh"][:], p1["w_hh"].rearrange("(g p) d -> p g d", p=P)), (raw["w_ih"][:], p1["w_ih"].rearrange("(g p) d -> p g d", p=P)),
            (raw["weight"][:], p1["weight"].rearrange("l d e -> d l e")),
            (w0_1[:], p0["W_1"]), (w0_2[:], p0["W_2"]),
            (raw["a_1"][:], p0["a_1"]), (raw["a_2"][:], p0["a_2"]),
            (raw["ai_w"][:], p3["ai_w"].rearrange("o p -> p o")), (raw["aj_w"][:], p3["aj_w"].rearrange("o p -> p o")),
            (raw["W_b"][:], column(p3["W_b"])), (bias3[:], everywhere(p3["W_b"], D)),
            (raw["aib"][:], everywhere(p3["ai_b"], 1)), (raw["ajb"][:], everywhere(p3["aj_b"], 1)),
        ]
        loads += [(raw["a2"][:, c:c + 1], p2["a"][c * P:(c + 1) * P, :]) for c in range(2)]
        for g in range(3):
            loads += [(b_ih[:, g:g + 1], column(p1["b_ih"][g * D:(g + 1) * D])), (b_hh[:, g:g + 1], column(p1["b_hh"][g * D:(g + 1) * D]))]
        N_LOADS = len(loads)

        UNITS = [(t, h) for h in range(H) for t in range(T)]
        NU = len(UNITS)
        Y_BANKS = (6, 7, 3)
        LESS = 2
        EARLY = 1
        LAG = 3

        def chain_steps(prev, L):
            s = []
            if prev in ("att0", "att2", "att3", "att3 and on"):
                s += [("mixed", 0), ("mixed", 1), ("below", 0), ("elu_exp", 0), ("below", 1), ("elu_exp", 1), ("x", 0)]
                if L in (None, "att0"):
                    s += [("x", 1)]
            if L is None:
                return s
            if prev == "att3 and on":
                s += ["pause"] * 4
            if L == "att0" or prev == "gru":
                s += [("stats", 0), ("stats", 1)]
            else:
                s += [("stats", 0), ("x", 1), ("stats", 1)]
            s += ["rstd", "pause", "shift"] + [("h_nat", t) for t in range(0, T, 2)]
            for h in range(H):
                s += [("turn", h), ("turned", h)]
            if L in ("att0", "gru"):
                s += [("split", h) for h in range(H)]
            if L == "gru":
                return s + ["part_hi", "part_lo"]
            for what in ("s", "vals", "q", "extra") if L == "att0" else ("s", "vals"):
                for h in range(H):
                    s += [(what, h), (what + "_out", h)]
            s += ["s_col", "pause", "s_col_out"]
            if L != "att0":
                s += ["s2"]
            s += [("top", t) for t in range(T)] + ["c_col", "c_cols", "c_row", "pause", "c_row_out"]
            return s

        def before(prev):
            return "att3" if prev == "att3 and on" else prev

        def part_of(prev, L, first=None, end=None):
            s = chain_steps(prev, L)
            return s[s.index(first) if first else 0:s.index(end) if end else len(s)]

        MIX, GRU = [(4, 5)], [(2, 3)]
        CUT1, CUT2, CUT3, CUT4 = ("x", 1), "part_lo", ("h_nat", 0), ("vals", 1)
        first_plan = [(None, (0, None, "att0"), [(4, 5), (6, 7)])]
        plan = [(("mix", 0, "att0"), (1, None, "att0"), MIX),
                (("mix", 1, "att0"), (0, "att0", "gru"), MIX),
                (("gather", 0, 0), (1, "att0", "gru", None, ("below", 0)), GRU),
                (("gates", 0, 0), (1, "att0", "gru", ("below", 0), CUT1), GRU),
                (("back", 0, 0), None, GRU),
                (("gather", 0, 1), (1, "att0", "gru", CUT1, CUT2), GRU),
                (("gates", 0, 1), (1, "att0", "gru", CUT2), GRU)]
        assert GRU_LAYERS >= 3
        for l in range(GRU_LAYERS - 1):
            if l:
                plan += [(("gates", 0, l + 1), None, GRU)]
            plan += [(("gather", 1, l), None, GRU), (("back", 0, l + 1), None, GRU)]
            if l < GRU_LAYERS - 2:
                plan += [(("gates", 1, l), None, GRU), (("gather", 0, l + 2), None, GRU), (("back", 1, l), None, GRU)]
        l = GRU_LAYERS - 2
        plan += [(("gates", 1, l), (0, "gru", "att2", None, CUT3), GRU),
                 (("back", 1, l), None, GRU),
                 (("gather", 1, l + 1), (0, "gru", "att2", CUT3, CUT4), GRU),
                 (("gates", 1, l + 1), (0, "gru", "att2", CUT4), GRU),
                 (("back", 1, l + 1), None, GRU),
                 (("mix", 0, "att2"), (1, "gru", "att2"), MIX),
                 (("mix", 1, "att2"), (0, "att2", "att3"), MIX),
                 (("mix", 0, "att3"), (1, "att2", "att3"), MIX)]
        last_plan = plan + [(("mix", 1, "att3"), (0, "att3", None), MIX),
                            (None, (1, "att3", None), MIX)]
        plan = plan + [(("mix", 1, "att3"), (0, "att3 and on", "att0", None, ("top", 0)), MIX),
                       (None, (1, "att3", None), MIX),
                       (None, (0, "att3 and on", "att0", ("top", 0)), [(4, 5), (6, 7)])]
        WEIGHT = {"mixed": 1.0, "below": 0.6, "elu_exp": 0.6, "x": 1.9, "stats": 1.4, "rstd": 1.0, "shift": 1.5, "h_nat": 0.8, "turn": 0.3,
                  "turned": 0.9, "split": 1.5, "part_hi": 0.6, "part_lo": 0.3, "s": 0.5, "s_out": 0.7, "vals": 0.3, "vals_out": 0.7, "q": 0.7,
                  "q_out": 1.0, "extra": 0.7, "extra_out": 0.7, "s_col": 1.0, "s_col_out": 0.1, "s2": 0.8, "top": 1.3, "c_col": 0.4, "c_cols": 0.1,
                  "c_row": 2.0, "c_row_out": 1.9, "pause": 1.2}

        PACE = {("gates", 0, 0): 1.15, ("gather", 0, 1): 0.65, ("gates", 0, 1): 1.27, ("gather", 1, 2): 0.74,
                ("mix", 0, "att2"): 1.15, ("mix", 1, "att2"): 0.7, ("mix", 0, "att3"): 0.7, ("mix", 1, "att3"): 1.15}

        def weight(step):
            return WEIGHT[step[0] if isinstance(step, tuple) else step]

        MAIN_STEPS = {"mix": NU + LAG, "gather": H * T // 2, "gates": 5 * H, "back": H}

        def run(plan, mains, chain):
            late = []
            for (main, beside, banks), (then, _, _) in zip(plan, plan[1:] + [(None, None, None)]):
                todo = part_of(*beside[1:]) if beside else []
                then_late = []
                if main and then and then[0] == "mix" and "c_col" in todo:
                    at = todo.index("c_col")
                    todo, then_late = todo[:at], [(beside[:3], step) for step in todo[at:]]
                whole, given, spent = sum(weight(step) for step in todo), 0, 0.0
                if main:
                    stage = mains[main[0]](*main[1:])
                    n = MAIN_STEPS[main[0]]
                    for m in range(n):
                        next(stage)
                        if m == EARLY - 1:
                            for of_chain, step in late:
                                chain(*of_chain, banks, step)
                            late = []
                        while given < len(todo) and spent < whole * ((m + 1) / n) ** PACE.get(main, 1.0):
                            chain(*beside[:3], banks, todo[given])
                            spent += weight(todo[given])
                            given += 1
                    next(stage, None)
                for step in todo[given:]:
                    chain(*beside[:3], banks, step)
                late = late + then_late

        def sum_bank(k, l, h):
            return (7, 5)[h] if (k, l) == (0, 0) else h

        def y_bank(u):
            return Y_BANKS[u % 3]

        def ring_at(u):
            return ring[:, u % RING, :]

        plan_of_gates = [(m[1], m[2], h) for m, _, _ in plan if m and m[0] == "gates" for h in range(H)]
        norms = [(beside[0], beside[2]) for _, beside, _ in plan if beside and ("stats", 0) in part_of(*beside[1:])]
        previous = dict(zip(norms[1:], norms))

        def passes(engine, run_plan):
            counted = (pe_s, act_s, dve_s, pool_s)

            def begin(phase):
                for s in counted:
                    s.begin(phase)

            def end(n):
                engine.drain().then_inc(arrived, 1)
                engine.wait_ge(go, n)

            begin("first")
            run_plan(first_plan, -1)
            end(1)
            begin("loop")
            with engine.Fori(0, PAIRS - 1) as pair:
                run_plan(plan, pair)
                end(pair + 2)
            begin("last")
            run_plan(last_plan, PAIRS - 1)

        def bank(b):
            return psum[:, b, :]

        def tile_of(ap, t):
            return ap[:, t * P:(t + 1) * P]

        def half_of(ap, h):
            return ap[:, h * HALF:(h + 1) * HALF]

        def acc(t):
            return psum[:, t // 3, (t % 3) * VW:(t % 3 + 1) * VW]

        def flat(ap):
            return ap.rearrange("p t d -> p (t d)")

        h_flat = flat(h_nat[:])
        unkept = [h_flat.bitcast(BF16)[:, n * N:(n + 1) * N] for n in range(2)]
        ATT = {"att0": 0, "att2": 1, "att3": 2}

        block = ctx.enter_context(nc.Block())

        @block.tensor
        def _(pe):
            pe.wait_ge(*ident_ready.at("ident"))
            pe.wait_ge(loaded_w, 16 * N_LOADS)

            def tr(b, src):
                return pe.transpose(bank(b)[:, 0:P], src, ident[:])

            tr(0, raw["W0"][:]).then_inc(*setup_pe.done("W0T"))
            tr(1, raw["W3"][:]).then_inc(*setup_pe.done("W3"))
            tr(2, raw["W2"][:]).then_inc(*setup_pe.done("W2T"))
            for g in range(3):
                tr(3 + g, raw["w_hh"][:, g, :]).then_inc(*setup_pe.done("w_hh", g))
            pe.wait_ge(*weights.at("copies1"))
            for g in range(3):
                tr(3 + g, raw["w_ih"][:, g, :]).then_inc(*setup_pe.done("w_ih", g))
            for l in range(GRU_LAYERS):
                tr(l, raw["weight"][:, l, :]).then_inc(*setup_pe.done("weight", l))
            pe.wait_ge(*weights.at("copies2"))
            for l in range(GRU_LAYERS):
                pe.matmul(bank(l)[:, 0:3 * D], raw["weightT"][:, l, :], raw["w_ihT"][:], start=True, stop=True).then_inc(*setup_pe.done("wg_in", l))
            pe.matmul(bank(3)[:, 0:P], raw["a_12"][:], raw["W0T"][:], start=True, stop=True).then_inc(*setup_pe.done("a12W"))
            pe.matmul(bank(4)[:, 1:2], raw["W0T"][:], raw["a_2"][:], start=True, stop=True)
            pe.matmul(bank(4)[:, 2:3], raw["W0T"][:], raw["a_1"][:], start=True, stop=True)
            pe.matmul(bank(4)[:, 3:4], raw["W2T"][:], raw["a2"][:, 0:1], start=True, stop=True)
            pe.matmul(bank(4)[:, 4:5], raw["W2T"][:], raw["a2"][:, 1:2], start=True, stop=True)
            pe.matmul(bank(4)[:, 5:6], raw["W3"][:], raw["ai_w"][:], start=True, stop=True)
            pe.matmul(bank(4)[:, 6:7], raw["W3"][:], raw["aj_w"][:], start=True, stop=True)
            pe.matmul(bank(4)[:, 7:8], raw["b_rep"][:], raw["aij"][:], start=True, stop=True).then_inc(*setup_pe.done("vectors"))
            pe.wait_ge(*weights.at("copies3"))
            pe.matmul(bank(5)[:, 0:P], raw["a12WT"][:], raw["W0T"][:], start=True, stop=True).then_inc(*setup_pe.done("g0"))
            pe.wait_ge(*weights.at("all"))

            busy = {}

            def take(*banks):
                for b in banks:
                    if b in busy:
                        pe.wait_ge(*busy.pop(b))

            def three(to, a, b, start=True, stop=True, group=True):
                (a_hi, a_lo), (b_hi, b_lo) = a, b
                pe.matmul(to, a_hi, b_hi, start=start, stop=False, skip_group_check=not group)
                pe.matmul(to, a_hi, b_lo, start=False, stop=False, skip_group_check=not group)
                return pe.matmul(to, a_lo, b_hi, start=False, stop=stop, skip_group_check=not group)

            def chain(k, prev, L, pairs, step):
                prev = before(prev)
                b0, b1 = pairs[0]
                what, h = step if isinstance(step, tuple) else (step, None)
                hT = (hT_hi[k], hT_lo[k])
                b = (b0, b1)[h] if h in range(H) else None
                if what == "turn":
                    take(b)
                    for t in range(h * TH, (h + 1) * TH):
                        pe.wait_ge(*act_s.at("h_nat", k, L, t))
                        m = pe.transpose(tile_of(bank(b), t - h * TH), h_nat[:, t, :], ident[:])
                    m.then_inc(*pe_s.done("turn", k, L, h))
                    busy[b] = act_s.at("hT", k, L, h)
                if what == "s":
                    take(b)
                    pe.wait_ge(*act_s.at("hT", k, L, h))
                    pe.matmul(psum[S_ROWS, b, :], v_s[:, ATT[L], :], half_of(extra[k], h), start=True, stop=True).then_inc(*pe_s.done("s", k, L, h))
                    busy[b] = dve_s.at("s2_row", k, L, h)
                if what in ("vals", "extra"):
                    take(b)
                    w = {"att0": w0_2 if what == "vals" else w0_1, "att2": w2, "att3": w3}[L]
                    for t in range(h * TH, (h + 1) * TH):
                        m = pe.matmul(tile_of(bank(b), t - h * TH), tile_of(extra[k], t), w[:], start=True, stop=True)
                    m.then_inc(*pe_s.done(what, k, L, h))
                    busy[b] = dve_s.at("vals", k, L, h) if L == "att3" else act_s.at(what, k, L, h)
                if what == "q":
                    take(b)
                    pe.wait_ge(*dve_s.at("hT_lo", k, L, h))
                    three(bank(b), (g0[0][:], g0[1][:]), (half_of(hT[0], h), half_of(hT[1], h))).then_inc(*pe_s.done("q", k, h))
                    busy[b] = dve_s.at("q_lo", k, h)
                if what == "s_col":
                    take(b0)
                    for h in range(H):
                        pe.wait_ge(*dve_s.at("s1_row", k, L, h))
                    for t in range(T):
                        m = pe.transpose(psum[:, b0, 2 * t:2 * t + 2], tile_of(rows_i[k][S1, :], t).bitcast(F32), ident[S1, S1])
                    m.then_inc(*pe_s.done("s_col", k, L))
                    busy[b0] = dve_s.at("s_col", k, L)
                if what == "s2":
                    for h in range(H):
                        b = (b0, b1)[h]
                        take(b)
                        pe.wait_ge(*dve_s.at("s2_row", k, L, h))
                        m = pe.matmul(bank(b), rows_i[k][S2, 0:P], half_of(rows_j[k][S2, :], h), start=True, stop=True)
                        busy[b] = dve_s.at("top", k, L, T - 1)
                    m.then_inc(*pe_s.done("s2", k, L))
                if what == "top" and L == "att0":
                    t = h
                    b = pairs[t % len(pairs)]
                    for h in range(H):
                        if t == 0:
                            pe.wait_ge(*dve_s.at("q_lo", k, h))
                        take(b[h])
                        three(bank(b[h]), (tile_of(part_hi[k], t), tile_of(part_lo[k], t)), (half_of(hT[0], h), half_of(hT[1], h))).then_inc(*pe_s.done("qh", k, t, h))
                        busy[b[h]] = dve_s.at("top", k, L, t, h)
                if what == "c_row":
                    pe.wait_ge(*dve_s.at("c_cols", k, L))
                    for h in range(H):
                        b = (b0, b1)[h]
                        take(b)
                        for t in range(h * TH, (h + 1) * TH):
                            m = pe.transpose(psum[0:2, b, (t - h * TH) * P:(t - h * TH + 1) * P], c_cols[k][:, t, :].bitcast(F32), ident[:])
                        m.then_inc(*pe_s.done("c_row", k, L, h))
                        busy[b] = act_s.at("c_row", k, L, h)

            def mix(k, L):
                ready = (k, L) != (0, "att0")
                if (k, L) == (1, "att0"):
                    pe.wait_ge(*dve_s.at("mask", k, T - 1))

                rows = {"att0": S1, "att2": ALL_ROWS, "att3": S_ROWS}[L]

                def logits(u):
                    t, h = UNITS[u]
                    b = y_bank(u)
                    take(b)
                    for i in range(TH):
                        pe.matmul(tile_of(bank(b), i), tile_of(mask[k][:, h * TH + i, :], t), ident_b[:],
                                  start=i == 0, stop=False, skip_group_check=True)
                    if L == "att0":
                        three(bank(b), (tile_of(hT_hi[k], t), tile_of(hT_lo[k], t)), (half_of(part_hi[k], h), half_of(part_lo[k], h)),
                              start=False, stop=False, group=False)
                    r = S_ROWS if L == "att2" and u < EARLY else rows
                    m = pe.matmul(bank(b), tile_of(rows_j[k][r, :], t), half_of(rows_i[k][r, :], h), start=False, stop=True, skip_group_check=True)
                    if r == rows:
                        m.then_inc(*pe_s.done("logits", k, L, u))
                    busy[b] = act_s.at("probs", k, L, u) if L == "att2" else dve_s.at("leaky", k, L, u)

                def less_top(u):
                    t, h = UNITS[u]
                    if ready and u == 0:
                        for half in range(H):
                            pe.wait_ge(*act_s.at("c_row", k, L, half))
                    if L != "att2":
                        pe.wait_ge(*act_s.at("relu", k, L, u))
                    m = pe.matmul(bank(y_bank(u)), tile_of(rows_j[k][C, :], t), half_of(rows_i[k][C, :], h), start=False, stop=True, skip_group_check=True)
                    m.then_inc(*pe_s.done("logits" if L == "att2" else "less_top", k, L, u))

                def weigh(u):
                    t, h = UNITS[u]
                    pe.wait_ge(*act_s.at("probs", k, L, u))
                    if u == 0:
                        for half in range(H) if ready else ():
                            pe.wait_ge(*(dve_s if L == "att3" else act_s).at("vals", k, L, half))
                        take(0, 1, 2)
                    for i in range(TH):
                        o = h * TH + i
                        m = pe.matmul(acc(o), tile_of(ring_at(u), i), vals[k][:, t, :], start=t == 0 and o % 3 == 0, stop=t == T - 1, skip_group_check=True)
                    m.then_inc(*pe_s.done("weighed", k, L, u))

                for s in range(NU + LAG):
                    if L != "att2" and 0 <= s - LESS < NU:
                        less_top(s - LESS)
                    if L == "att2" and s == EARLY:
                        for u in range(EARLY):
                            less_top(u)
                    if s < NU:
                        logits(s)
                    if s >= LAG:
                        weigh(s - LAG)
                    if s == NU + LAG - 1:
                        for b in range(3):
                            busy[b] = dve_s.at("mixed", k, L, H - 1)
                    yield

            def gather(k, l):
                for h in range(H):
                    b = sum_bank(k, l, h)
                    take(b)
                    for t in range(T):
                        if h == 0 and l == 0:
                            pe.wait_ge(*pool_s.at("edges", k, t))
                            if t == 0:
                                pe.wait_ge(*dve_s.at("part_lo", k, "gru"))
                        elif h == 0 and t % TH == 0:
                            pe.wait_ge(*act_s.at("nat_hi", k, l - 1, t // TH))
                            pe.wait_ge(*dve_s.at("nat_lo", k, l - 1, t // TH))
                        for part in (part_hi, part_lo):
                            m = pe.matmul(bank(b), tile_of(part[k], t), edges[k][:, t, h * HALF:(h + 1) * HALF],
                                          start=t == 0 and part is part_hi, stop=t == T - 1 and part is part_lo)
                        if t == T - 1:
                            m.then_inc(*pe_s.done("sum", k, l, h))
                            busy[b] = dve_s.at("sum_lo", k, l, h)
                        if t % 2:
                            yield

            def gates(k, l):
                for h in range(H):
                    if l == 0:
                        pe.wait_ge(*dve_s.at("hT_lo", k, "gru", h))
                    else:
                        pe.wait_ge(*act_s.at("state_hi", k, l - 1, h))
                        pe.wait_ge(*pool_s.at("state_lo", k, l - 1, h))
                    inp = (half_of(sum_hi[k], h), half_of(sum_lo[k], h))
                    hid = (half_of(hT_hi[k], h), half_of(hT_lo[k], h))

                    def w_in(g):
                        return tuple(w[:, l, g * D:(g + 1) * D] for w in wg_in)

                    def w_h(g):
                        return tuple(w[:, g * D:(g + 1) * D] for w in wg_h)

                    take(6)
                    three(bank(6), w_h(2), hid).then_inc(*pe_s.done("gate", k, l, h, 2))
                    busy[6] = act_s.at("gate", k, l, h, 2)
                    for g in range(2):
                        take(4 + g)
                        three(bank(4 + g), w_h(g), hid, stop=False)
                        if g == 0:
                            pe.wait_ge(*dve_s.at("sum_lo", k, l, h))
                        three(bank(4 + g), w_in(g), inp, start=False).then_inc(*pe_s.done("gate", k, l, h, g))
                        busy[4 + g] = act_s.at("gate", k, l, h, g)
                    yield
                    take(7)
                    three(bank(7), w_in(2), inp).then_inc(*pe_s.done("gate", k, l, h, 3))
                    busy[7] = dve_s.at("n_sum", k, l, h)
                    for _ in range(4):
                        yield

            def back(k, l):
                for h in range(H):
                    pe.wait_ge(*dve_s.at("state", k, l, h))
                    take(h)
                    for i in range(TH):
                        m = pe.transpose(tile_of(bank(h), i), tile_of(extra[k], h * TH + i), ident[:])
                    m.then_inc(*pe_s.done("nat", k, l, h))
                    busy[h] = dve_s.at("nat_lo", k, l, h) if l < GRU_LAYERS - 1 else dve_s.at("x_gru", k, h)
                    yield

            def run_plan(plan, pair):
                busy.clear()
                run(plan, {"mix": mix, "gather": gather, "gates": gates, "back": back}, chain)

            passes(pe, run_plan)

        @block.scalar
        def _(act):
            for dst, src in loads[1::2]:
                act.dma_start(dst, src).then_inc(loaded_w, 16)

            def chain(k, prev, L, pairs, step):
                prev = before(prev)
                b0, b1 = pairs[0]
                what, h = step if isinstance(step, tuple) else (step, None)
                if what == "below":
                    act.wait_ge(*dve_s.at("mixed", k, prev, h))
                    act.activation(half_of(h_flat, h), half_of(extra[k], h), ACT.Relu, scale=-1.0).then_inc(*act_s.done("below", k, prev, h))
                if what == "elu_exp":
                    act.wait_ge(*act_s.at("below", k, prev, h))
                    act.activation(half_of(h_flat, h), half_of(h_flat, h), ACT.Exp, scale=-1.0).then_inc(*act_s.done("elu_exp", k, prev, h))
                if what == "h_nat":
                    if h == 0:
                        act.wait_ge(*dve_s.at("shift", k, L))
                    for t in (h, h + 1):
                        act.activation(h_nat[:, t, :], xs[k][:, t, :], ACT.Relu, bias=shift[:, t:t + 1], scale=rstd[:, t:t + 1]).then_inc(*act_s.done("h_nat", k, L, t))
                if what == "turned":
                    act.wait_ge(*pe_s.at("turn", k, L, h))
                    act.activation(half_of(extra[k], h), bank((b0, b1)[h]), ACT.Copy).then_inc(*act_s.done("hT", k, L, h))
                if what == "s_out":
                    if L == "att3":
                        act.wait_ge(*dve_s.at("s_biased", k, h))
                    act.wait_ge(*pe_s.at("s", k, L, h))
                    act.activation(half_of(s_hi[S_ROWS, :], h), psum[S_ROWS, (b0, b1)[h], :], ACT.Copy).then_inc(*act_s.done("s_hi", k, L, h))
                if what == "vals_out" and L != "att3":
                    act.wait_ge(*pe_s.at("vals", k, L, h))
                    act.activation(vals[k][:, h * TH:(h + 1) * TH, 0:D], bank((b0, b1)[h]).rearrange("p (t d) -> p t d", d=D), ACT.Copy).then_inc(*act_s.done("vals", k, L, h))
                if what == "q_out":
                    act.wait_ge(*pe_s.at("q", k, h))
                    act.activation(half_of(part_hi[k], h), bank((b0, b1)[h]), ACT.Identity, bias=v0_s2).then_inc(*act_s.done("q_hi", k, h))
                if what == "extra_out":
                    act.wait_ge(*pe_s.at("extra", k, L, h))
                    act.activation(half_of(extra[k], h), bank((b0, b1)[h]), ACT.Copy).then_inc(*act_s.done("extra", k, L, h))
                if what == "c_row_out":
                    for h in range(H):
                        act.wait_ge(*pe_s.at("c_row", k, L, h))
                        act.activation(half_of(rows_i[k][C, :], h), psum[0:2, (b0, b1)[h], :], ACT.Copy).then_inc(*act_s.done("c_row", k, L, h))

            def mix(k, L):
                if L == "att2" and k == 0:
                    act.wait_ge(*dve_s.at("state", 1, GRU_LAYERS - 1, H - 1))

                def ring_free(u):
                    if u >= RING:
                        act.wait_ge(*pe_s.at("weighed", k, L, u - RING))

                for s in range(NU + LAG):
                    y, p = ring_at(s), ring_at(s - LESS)
                    if L != "att2" and 0 <= s - LESS < NU:
                        act.wait_ge(*dve_s.at("leaky", k, L, s - LESS))
                        act.activation(p, p, ACT.Exp, scale=ALPHA).then_inc(*act_s.done("probs", k, L, s - LESS))
                    if L == "att2":
                        for u in range(EARLY + 1) if s == EARLY else (s,) if EARLY < s < NU else ():
                            act.wait_ge(*pe_s.at("logits", k, L, u))
                            ring_free(u)
                            act.activation(ring_at(u), bank(y_bank(u)), ACT.Exp).then_inc(*act_s.done("probs", k, L, u))
                    elif s < NU:
                        act.wait_ge(*pe_s.at("logits", k, L, s))
                        ring_free(s)
                        act.activation(y, bank(y_bank(s)), ACT.Relu, scale=STEEP).then_inc(*act_s.done("relu", k, L, s))
                    yield

            def gather(k, l):
                for _ in range(MAIN_STEPS["gather"]):
                    yield
                for h in range(H):
                    act.wait_ge(*pe_s.at("sum", k, l, h))
                    act.activation(half_of(sum_hi[k], h), bank(sum_bank(k, l, h)), ACT.Copy).then_inc(*act_s.done("sum_hi", k, l, h))

            def gates(k, l):
                for h in range(H):
                    at = plan_of_gates.index((k, l, h))
                    if at:
                        act.wait_ge(*dve_s.at("state", *plan_of_gates[at - 1]))
                    act.wait_ge(*pe_s.at("gate", k, l, h, 2))
                    act.activation(gru_hn, bank(6), ACT.Identity, bias=gate_bias[:, 2:3], scale=0.5).then_inc(*act_s.done("gate", k, l, h, 2))
                    act.wait_ge(*pe_s.at("gate", k, l, h, 0))
                    act.activation(gru_r, bank(4), ACT.Tanh, bias=gate_bias[:, 0:1], scale=0.5).then_inc(*act_s.done("gate", k, l, h, 0))
                    act.wait_ge(*pe_s.at("gate", k, l, h, 1))
                    act.activation(gru_z, bank(5), ACT.Tanh, bias=gate_bias[:, 1:2], scale=0.5).then_inc(*act_s.done("gate", k, l, h, 1))
                    yield
                    yield
                    act.wait_ge(*dve_s.at("n_sum", k, l, h))
                    act.activation(gru_n, gru_hn, ACT.Tanh, bias=gate_bias[:, 3:4]).then_inc(*act_s.done("n", k, l, h))
                    yield
                    yield
                    if l < GRU_LAYERS - 1:
                        act.wait_ge(*dve_s.at("state", k, l, h))
                        act.activation(half_of(hT_hi[k], h), half_of(extra[k], h), ACT.Copy).then_inc(*act_s.done("state_hi", k, l, h))
                    yield

            def back(k, l):
                for h in range(H):
                    if l < GRU_LAYERS - 1:
                        act.wait_ge(*pe_s.at("nat", k, l, h))
                        act.activation(half_of(part_hi[k], h), bank(h), ACT.Copy).then_inc(*act_s.done("nat_hi", k, l, h))
                    yield

            passes(act, lambda plan, pair: run(plan, {"mix": mix, "gather": gather, "gates": gates, "back": back}, chain))

        @block.vector
        def _(dve):
            def split(dst, src, *name):
                dve.tensor_copy(dst[0], src).then_inc(*weights.done(*name, "hi"))
                dve.wait_ge(*weights.last())
                dve.tensor_tensor(dst[1], src, dst[0].bitcast(F32), ALU.subtract).then_inc(*weights.done(*name))

            def copy_w(dst, src, step, label=None):
                dve.wait_ge(*setup_pe.at(*step))
                dve.tensor_copy(dst, src).then_inc(*weights.done(*(label or ("copied",) + step)))

            dve.memset(v_s[:], 0.0).then_inc(*weights.done("v_s", "zero"))
            dve.memset(lo_row[:], 0.0).then_inc(*weights.done("lo_row", "zero"))
            dve.memset(const3[:], 0.0).then_inc(*weights.done("const3", "zero"))
            for k in SLOTS:
                for rows in (rows_i[k], rows_j[k]):
                    dve.memset(rows[:].bitcast(F32), 0.0).then_inc(*weights.done("rows", "zero"))
            dve.wait_ge(*weights.last())
            for k in SLOTS:
                for to, pair in ((rows_j, S1), (rows_i, S2), (rows_j, C)):
                    dve.memset(to[k][pair, :].bitcast(F32), 1.0).then_inc(*weights.done("rows", "one"))
            for pair in (S1, S2):
                dve.memset(lo_row[pair, :], 1.0).then_inc(*weights.done("lo_row", "one"))
            dve.wait_ge(*weights.last())
            for k in SLOTS:
                for to, pair in ((rows_j, S1), (rows_i, S2)):
                    dve.memset(to[k][pair.start:pair.start + 1, :].bitcast(F32), -1.0).then_inc(*weights.done("rows", "minus"))
            for pair in (S1, S2):
                dve.memset(lo_row[pair.start:pair.start + 1, :], 0.0).then_inc(*weights.done("lo_row"))
            dve.wait_ge(loaded_w, 16 * N_LOADS)
            dve.wait_ge(*ident_ready.at("ident"))
            dve.tensor_copy(ident_b[:], ident[:]).then_inc(*weights.done("ident_b"))
            dve.tensor_copy(raw["b_rep"][:], raw["W_b"][:].broadcast_to([P, P])).then_inc(*weights.done("b_rep"))
            dve.tensor_tensor(raw["aij"][:], raw["ai_w"][:], raw["aj_w"][:], ALU.add).then_inc(*weights.done("aij"))
            for g in range(2):
                dve.tensor_scalar(gate_bias[:, g:g + 1], b_ih[:, g:g + 1], b_hh[:, g:g + 1], 0.5, ALU.add, ALU.mult).then_inc(*weights.done("gate_bias", g))
            dve.tensor_scalar(gate_bias[:, 2:3], b_hh[:, 2:3], 0.5, None, ALU.mult).then_inc(*weights.done("gate_bias", 2))
            dve.tensor_copy(gate_bias[:, 3:4], b_ih[:, 2:3]).then_inc(*weights.done("gate_bias", 3))
            copy_w(raw["W0T"][:], bank(0)[:, 0:P], ("W0T",))
            copy_w(w3[:], bank(1)[:, 0:P], ("W3",))
            dve.tensor_copy(w2[:], raw["W2"][:]).then_inc(*weights.done("w2"))
            copy_w(raw["W2T"][:], bank(2)[:, 0:P], ("W2T",))
            for g in range(3):
                dve.wait_ge(*setup_pe.at("w_hh", g))
                split(tuple(w[:, g * D:(g + 1) * D] for w in wg_h), bank(3 + g)[:, 0:P], "copies1")
            for g in range(3):
                copy_w(raw["w_ihT"][:, g * D:(g + 1) * D], bank(3 + g)[:, 0:P], ("w_ih", g))
            for l in range(GRU_LAYERS):
                copy_w(raw["weightT"][:, l, :], bank(l)[:, 0:P], ("weight", l), ("copies2",))
            for l in range(GRU_LAYERS):
                dve.wait_ge(*setup_pe.at("wg_in", l))
                split(tuple(w[:, l, :] for w in wg_in), bank(l)[:, 0:3 * D], "wg_in", l)
            copy_w(raw["a12WT"][:], bank(3)[:, 0:P], ("a12W",), ("copies3",))
            dve.wait_ge(*setup_pe.at("vectors"))
            for at, c in ((0, 0), (1, 0), (32, 1), (33, 1)):
                dve.tensor_copy(v_s[:, :, at], psum[:, 4, 1:7].rearrange("p (l c) -> p l c", c=2)[:, :, c]).then_inc(*weights.done("v_s"))
            dve.tensor_scalar(const3[S1, :], psum[S1, 4, 7:8], raw["aib"][S1, 0:1], raw["ajb"][S1, 0:1], ALU.add, ALU.add).then_inc(*weights.done("const3"))
            dve.wait_ge(*setup_pe.at("g0"))
            split((g0[0][:], g0[1][:]), bank(5)[:, 0:P], "g0")
            dve.engine_nop().then_inc(*weights.done("all"))
            dve.wait_ge(*weights.last())

            def chain(k, prev, L, pairs, step):
                prev = before(prev)
                b0, b1 = pairs[0]
                what, h = step if isinstance(step, tuple) else (step, None)
                xk = flat(xs[k][:])
                if what == "mixed":
                    if h == 0:
                        dve.wait_ge(*pe_s.at("weighed", k, prev, NU - 1))
                        for b in range(3):
                            n = min(3, T - 3 * b)
                            s = psum[:, b, 0:n * VW].rearrange("p (t w) -> p t w", w=VW)[:, :, D]
                            m = dve.reciprocal(rsum[k][:, 3 * b:3 * b + n], s)
                        m.then_inc(*dve_s.done("rsum", k, prev))
                        dve.wait_ge(*dve_s.last())
                    for t in range(h * TH, (h + 1) * TH):
                        dst = tile_of(extra[k], t)
                        if prev == "att0":
                            m = dve.scalar_tensor_tensor(dst, acc(t)[:, 0:D], rsum[k][:, t:t + 1], dst, ALU.mult, ALU.add)
                        else:
                            m = dve.tensor_scalar(dst, acc(t)[:, 0:D], rsum[k][:, t:t + 1], None, ALU.mult)
                    m.then_inc(*dve_s.done("mixed", k, prev, h))
                if what == "x":
                    xh = half_of(xk, h)
                    dve.wait_ge(*act_s.at("elu_exp", k, prev, h))
                    dve.scalar_tensor_tensor(xh, half_of(h_flat, h), -1.0, xh, ALU.add, ALU.add).then_inc(*dve_s.done("x_part", k, prev, h))
                    dve.wait_ge(*dve_s.last())
                    dve.scalar_tensor_tensor(xh, half_of(extra[k], h), 0.0, xh, ALU.max, ALU.add).then_inc(*dve_s.done("x", k, prev, h))
                if what == "stats":
                    if L == "att0":
                        dve.wait_ge(x_in[k], 16 * of_pass["loaded"][k])
                    else:
                        dve.wait_ge(*(dve_s.at("x_gru", k, h) if prev == "gru" else dve_s.at("x", k, prev, h)))
                    for t in range(h * TH, (h + 1) * TH):
                        m = dve.bn_stats(stats[:, t, :], xs[k][:, t, :])
                    m.then_inc(*dve_s.done("stats", k, L, h))
                if what == "rstd":
                    dve.wait_ge(*dve_s.at("stats", k, L, H - 1))
                    for t in range(T):
                        m = dve.bn_aggr(mean_var[:, t, :], stats[:, t, :])
                    m.then_inc(*dve_s.done("mean_var", k, L))
                if what == "shift":
                    dve.wait_ge(*pool_s.at("rstd", k, L))
                    if (k, L) in previous and dve_s.phase != "first":
                        pk, pL = previous[(k, L)]
                        dve.wait_ge(*act_s.at("h_nat", pk, pL, T - 1))
                    dve.scalar_tensor_tensor(shift[:], mean_var[:, :, 0], -1.0, rstd[:], ALU.mult, ALU.mult).then_inc(*dve_s.done("shift", k, L))
                    if L == "att0" and k == 0 and dve_s.phase == "first":
                        masks(k, range(T))
                if what == "part_hi":
                    dve.wait_ge(*act_s.at("h_nat", k, L, T - 1))
                    dve.tensor_copy(part_hi[k][:], h_flat).then_inc(*dve_s.done("part_hi", k, L))
                if what == "part_lo":
                    dve.wait_ge(*dve_s.at("part_hi", k, L))
                    dve.tensor_tensor(part_lo[k][:], h_flat, part_hi[k][:].bitcast(F32), ALU.subtract).then_inc(*dve_s.done("part_lo", k, L))
                if what == "turned" and L == "att0" and k == 1:
                    masks(k, range(h * TH, (h + 1) * TH))
                if what == "split":
                    dve.wait_ge(*act_s.at("hT", k, L, h))
                    dve.tensor_copy(half_of(hT_hi[k], h), half_of(extra[k], h)).then_inc(*dve_s.done("hT_hi", k, L, h))
                    dve.wait_ge(*dve_s.last())
                    dve.tensor_tensor(half_of(hT_lo[k], h), half_of(extra[k], h), half_of(hT_hi[k], h).bitcast(F32), ALU.subtract).then_inc(*dve_s.done("hT_lo", k, L, h))
                if what == "s_out":
                    b = (b0, b1)[h]
                    if L == "att3":
                        dve.wait_ge(*pe_s.at("s", k, L, h))
                        dve.tensor_scalar(psum[S_ROWS, b, :], psum[S_ROWS, b, :], const3[S_ROWS, 0:1], None, ALU.add).then_inc(*dve_s.done("s_biased", k, h))
                    dve.wait_ge(*act_s.at("s_hi", k, L, h))
                    for to, pair, name in ((rows_i, S1, "s1_row"), (rows_j, S2, "s2_row")):
                        dve.scalar_tensor_tensor(half_of(to[k][pair, :], h), psum[pair, b, :], lo_row[pair, 0:1], half_of(s_hi[pair, :], h).bitcast(F32),
                                                 ALU.mult, ALU.subtract).then_inc(*dve_s.done(name, k, L, h))
                if what == "s_col_out":
                    dve.wait_ge(*pe_s.at("s_col", k, L))
                    two = psum[:, b0, 0:2 * T].rearrange("p (t c) -> p t c", c=2)
                    dve.tensor_copy(s_col[k][:], two[:, :, 0]).then_inc(*dve_s.done("s_col_hi", k, L))
                    dve.wait_ge(*dve_s.last())
                    dve.tensor_tensor(s_col[k][:], two[:, :, 1], s_col[k][:], ALU.subtract).then_inc(*dve_s.done("s_col", k, L))
                if what == "vals_out":
                    if h == 0:
                        dve.memset(vals[k][:, :, D:VW], 1.0).then_inc(*dve_s.done("ones", k, L))
                    if L == "att3":
                        r = slice(h * TH, (h + 1) * TH)
                        dve.wait_ge(*pe_s.at("vals", k, L, h))
                        dve.tensor_tensor(vals[k][:, r, 0:D], bank((b0, b1)[h]).rearrange("p (t d) -> p t d", d=D),
                                          bias3[:].rearrange("p (o d) -> p o d", o=1).broadcast_to([P, TH, D]), ALU.add).then_inc(*dve_s.done("vals", k, L, h))
                if what == "q_out":
                    dve.wait_ge(*act_s.at("q_hi", k, h))
                    dve.scalar_tensor_tensor(half_of(part_lo[k], h), bank((b0, b1)[h]), v0_s2, half_of(part_hi[k], h).bitcast(F32), ALU.add, ALU.subtract).then_inc(*dve_s.done("q_lo", k, h))
                if what == "top":
                    t = h
                    if L == "att0":
                        if k == 0 and dve_s.phase != "first":
                            dve.wait_ge(*pool_s.at("mask", t))
                        for h in range(H):
                            b = pairs[t % len(pairs)][h]
                            dve.wait_ge(*pe_s.at("qh", k, t, h))
                            if t >= 1:
                                dve.wait_ge(*dve_s.at("top", k, L, t - 1, h))
                            dve.tensor_tensor_reduce(unkept[h][:, 0:HALF], bank(b), half_of(mask[k][:, t, :], h), 1.0, LOWEST,
                                                     ALU.add, ALU.max, top[k][:, t, h:h + 1]).then_inc(*dve_s.done("top", k, L, t, h))
                    else:
                        dve.wait_ge(*pe_s.at("s2", k, L))
                        if t >= 2:
                            dve.wait_ge(*dve_s.at("top", k, L, t - 2))
                        dve.tensor_tensor_reduce(unkept[t % 2], psum[:, b0:b0 + 2, :].rearrange("p b n -> p (b n)"), mask[k][:, t, :], 1.0, LOWEST,
                                                 ALU.add, ALU.max, top[k][:, t, 0:1]).then_inc(*dve_s.done("top", k, L, t))
                if what == "c_col":
                    dve.wait_ge(*(dve_s.at("top", k, L, T - 1, H - 1) if L == "att0" else dve_s.at("top", k, L, T - 1)))
                    best = top[k][:, :, 0]
                    if L == "att0":
                        for h in range(1, H):
                            dve.tensor_tensor(best, best, top[k][:, :, h], ALU.max).then_inc(*dve_s.done("best", k, L))
                            dve.wait_ge(*dve_s.last())
                    dve.tensor_tensor(best, best, s_col[k][:], ALU.add).then_inc(*dve_s.done("row_top", k, L))
                    dve.wait_ge(*dve_s.last())
                    if L == "att2":
                        dve.tensor_scalar(c_col[k][:], best, -1.0, None, ALU.mult).then_inc(*dve_s.done("c_col", k, L))
                    else:
                        dve.tensor_scalar(top2[k][:], best, 0.0, -STEEP, ALU.max, ALU.mult).then_inc(*dve_s.done("top2", k, L))
                        dve.wait_ge(*dve_s.last())
                        dve.tensor_tensor(c_col[k][:], top2[k][:], best, ALU.subtract).then_inc(*dve_s.done("c_col", k, L))
                if what == "c_cols":
                    dve.wait_ge(*dve_s.at("c_col", k, L))
                    to = c_cols[k]
                    dve.tensor_copy(to[:, :, 0], c_col[k][:]).then_inc(*dve_s.done("c_hi", k, L))
                    dve.wait_ge(*dve_s.last())
                    dve.tensor_tensor(to[:, :, 1], c_col[k][:], to[:, :, 0].bitcast(F32), ALU.subtract).then_inc(*dve_s.done("c_cols", k, L))

            def masks(k, tiles):
                for t in tiles:
                    if t % CHUNK == 0:
                        dve.wait_ge(adj_loaded[k][t // CHUNK], 16 * of_pass["loaded"][k])
                    dve.tensor_scalar(mask[k][:, t, :], adj_in[k][:, t, :], 0, MASKED, ALU.is_le, ALU.mult).then_inc(*dve_s.done("mask", k, t))

            def mix(k, L):
                for s in range(NU + LAG):
                    if L != "att2" and 0 <= s - LESS < NU:
                        u = s - LESS
                        dve.wait_ge(*pe_s.at("less_top", k, L, u))
                        dve.tensor_tensor(ring_at(u), bank(y_bank(u)), ring_at(u), ALU.add).then_inc(*dve_s.done("leaky", k, L, u))
                    yield

            def gather(k, l):
                for _ in range(MAIN_STEPS["gather"]):
                    yield
                for h in range(H):
                    dve.wait_ge(*act_s.at("sum_hi", k, l, h))
                    dve.tensor_tensor(half_of(sum_lo[k], h), bank(sum_bank(k, l, h)), half_of(sum_hi[k], h).bitcast(F32), ALU.subtract).then_inc(*dve_s.done("sum_lo", k, l, h))

            def gates(k, l):
                for h in range(H):
                    yield
                    dve.wait_ge(*act_s.at("gate", k, l, h, 0))
                    dve.scalar_tensor_tensor(gru_hn, gru_r, 1.0, gru_hn, ALU.add, ALU.mult).then_inc(*dve_s.done("r_n", k, l, h))
                    yield
                    dve.wait_ge(*pe_s.at("gate", k, l, h, 3))
                    dve.wait_ge(*dve_s.last())
                    dve.tensor_tensor(gru_hn, bank(7), gru_hn, ALU.add).then_inc(*dve_s.done("n_sum", k, l, h))
                    yield
                    dve.wait_ge(*act_s.at("n", k, l, h))
                    dve.tensor_tensor(gru_r, half_of(extra[k], h), gru_n, ALU.subtract).then_inc(*dve_s.done("h_less_n", k, l, h))
                    dve.wait_ge(*dve_s.last())
                    dve.scalar_tensor_tensor(gru_r, gru_z, 1.0, gru_r, ALU.add, ALU.mult).then_inc(*dve_s.done("z_part", k, l, h))
                    dve.wait_ge(*dve_s.last())
                    dve.scalar_tensor_tensor(half_of(extra[k], h), gru_r, 0.5, gru_n, ALU.mult, ALU.add).then_inc(*dve_s.done("state", k, l, h))
                    yield
                    yield

            def back(k, l):
                for h in range(H):
                    if l < GRU_LAYERS - 1:
                        dve.wait_ge(*act_s.at("nat_hi", k, l, h))
                        dve.tensor_tensor(half_of(part_lo[k], h), bank(h), half_of(part_hi[k], h).bitcast(F32), ALU.subtract).then_inc(*dve_s.done("nat_lo", k, l, h))
                    else:
                        dve.wait_ge(*pe_s.at("nat", k, l, h))
                        xk = half_of(flat(xs[k][:]), h)
                        dve.tensor_tensor(xk, bank(h), xk, ALU.add).then_inc(*dve_s.done("x_gru", k, h))
                    yield

            of_pass = {}

            def run_plan(plan, pair):
                of_pass["loaded"] = (pair + 2, pair + 1)
                run(plan, {"mix": mix, "gather": gather, "gates": gates, "back": back}, chain)

            passes(dve, run_plan)

        @block.gpsimd
        def _(pool):
            pool.memset(minus_half[:], -0.5).then_inc(*ident_ready.done("half"))
            pool.memset(ident[:], 0.0).then_inc(*ident_ready.done("zero"))
            pool.wait_ge(*ident_ready.last())
            pool.affine_select(out=ident[:], in_=ident[:], compare_op=ALU.not_equal, fill=1.0, base=0,
                               pattern=[[-1, P]], channel_multiplier=1).then_inc(*ident_ready.done("ident"))

            def chain(k, prev, L, pairs, step):
                if step == "shift":
                    pool.wait_ge(*dve_s.at("mean_var", k, L))
                    pool.tensor_scalar(rstd[:], mean_var[:, :, 1], EPS, 1.0, ALU.add, ALU.mult).then_inc(*pool_s.done("var", k, L))
                    pool.wait_ge(*pool_s.last())
                    pool.tensor_tensor(rstd[:], rstd[:], minus_half[:], ALU.pow).then_inc(*pool_s.done("rstd", k, L))
                    if k == 0 and L == "att0" and pool_s.phase != "first":
                        pool.wait_ge(*dve_s.at("mixed", k, "att3", H - 1))
                        for t in range(T):
                            if t % CHUNK == 0:
                                pool.wait_ge(adj_loaded[k][t // CHUNK], 16)
                            pool.tensor_scalar(mask[k][:, t, :], adj_in[k][:, t, :], 0, MASKED, ALU.is_le, ALU.mult).then_inc(*pool_s.done("mask", t))

            def mix(k, L):
                for s in range(NU + LAG):
                    t = s - T
                    if L == "att0" and 0 <= t < T:
                        if k == 1 and t == 0:
                            pool.wait_ge(*dve_s.at("mask", k, T - 1))
                        pool.tensor_scalar(edges[k][:, t, :], adj_in[k][:, t, :], 0, 0, ALU.is_equal, ALU.is_equal).then_inc(*pool_s.done("edges", k, t))
                    yield

            def gates(k, l):
                for h in range(H):
                    for _ in range(4):
                        yield
                    if l < GRU_LAYERS - 1:
                        pool.wait_ge(*dve_s.at("state", k, l, h))
                        pool.wait_ge(*act_s.at("state_hi", k, l, h))
                        pool.tensor_tensor(half_of(hT_lo[k], h), half_of(extra[k], h), half_of(hT_hi[k], h).bitcast(F32), ALU.subtract).then_inc(*pool_s.done("state_lo", k, l, h))
                    yield

            def nothing(name):
                def stage(*_):
                    for _ in range(MAIN_STEPS[name]):
                        yield
                return stage

            passes(pool, lambda plan, pair: run(plan, {"mix": mix, "gates": gates, **{name: nothing(name) for name in ("gather", "back")}}, chain))

        @block.sync
        def _(sp):
            def load_x(k, pair):
                sp.dma_start(xs[k][:], x.rearrange("g (t p) d -> g p t d", p=P)[bass.ds(2 * pair + k, 1)].rearrange("o p t d -> (o p) t d")).then_inc(x_in[k], 16)

            def load_adj(k, pair):
                g = adj.rearrange("g (t p) n -> g p t n", p=P)[bass.ds(2 * pair + k, 1)].rearrange("o p t n -> (o p) t n")
                for c in range(CHUNKS):
                    sp.dma_start(adj_in[k][:, c * CHUNK:(c + 1) * CHUNK, :], g[:, c * CHUNK:(c + 1) * CHUNK, :]).then_inc(adj_loaded[k][c], 16)

            def store(k, pair):
                sp.wait_ge(*dve_s.at("x", k, "att3", H - 1))
                sp.dma_start(out.rearrange("g (t p) d -> g p t d", p=P)[bass.ds(2 * pair + k, 1)].rearrange("o p t d -> (o p) t d"), xs[k][:]).then_inc(stored, 16)
                sp.wait_ge(stored, 16 * (k + 1))

            for k in SLOTS:
                load_x(k, 0)
            for dst, src in loads[0::2]:
                sp.dma_start(dst, src).then_inc(loaded_w, 16)
            load_adj(0, 0)
            sp.wait_ge(*weights.at("all"))
            load_adj(1, 0)

            def end():
                sp.wait_ge(arrived, 4)
                sp.sem_clear(range(per_pass[0].num, per_pass[-1].num + 1))
                sp.sem_inc(go, 1)

            def begin(phase):
                for s in (pe_s, dve_s):
                    s.begin(phase)

            end()
            begin("loop")
            with sp.Fori(0, PAIRS - 1) as pair:
                for k in SLOTS:
                    sp.wait_ge(*pe_s.at("sum", k, GRU_LAYERS - 1, H - 1))
                    load_adj(k, pair + 1)
                for k in SLOTS:
                    store(k, pair)
                    load_x(k, pair + 1)
                end()
            begin("last")
            for k in SLOTS:
                store(k, PAIRS - 1)


_ARGS = {
    "x": "x", "adj": "adj",
    "p0": {"W": "L0_gnn_W", "a_1": "L0_gnn_a_1", "a_2": "L0_gnn_a_2", "a_12": "L0_gnn_a_12", "W_1": "L0_gnn_W_1", "W_2": "L0_gnn_W_2"},
    "p1": {"weight": "L1_gnn_weight", "w_ih": "L1_gnn_w_ih", "w_hh": "L1_gnn_w_hh", "b_ih": "L1_gnn_b_ih", "b_hh": "L1_gnn_b_hh"},
    "p2": {"W": "L2_gnn_W", "a": "L2_gnn_a"},
    "p3": {"W_w": "L3_gnn_W_w", "W_b": "L3_gnn_W_b", "ai_w": "L3_gnn_ai_w", "ai_b": "L3_gnn_ai_b", "aj_w": "L3_gnn_aj_w", "aj_b": "L3_gnn_aj_b"},
}


def kernel(**inputs):
    import concourse.bacc as _bacc
    from concourse.bass_utils import run_bass_kernel_spmd as _run

    counts = {}
    for _ in range(2):
        nc = _bacc.Bacc("TRN2", target_bir_lowering=False, num_devices=1)
        arrays = {}

        def dram(name):
            a = np.ascontiguousarray(inputs[name])
            arrays[f"in_{name}"] = a
            return nc.dram_tensor(f"in_{name}", a.shape, mybir.dt.from_np(a.dtype), kind="ExternalInput").ap()

        args = {k: dram(v) if isinstance(v, str) else {n: dram(m) for n, m in v.items()} for k, v in _ARGS.items()}
        args["out"] = nc.dram_tensor("out_x", args["x"].shape, F32, kind="ExternalOutput").ap()
        build(nc, counts, **args)
    r = _run(nc, [arrays], core_ids=[0])
    return r.results[0]["out_x"]
```
